# Optimizing a Trainium2 kernel written in Bass

```python
import numpy as np
import jax
import jax.numpy as jnp

def _softmax(x, axis=-1):
    return jax.nn.softmax(x, axis=axis)

def _gelu(x):
    return jax.nn.gelu(x, approximate=True)

def _silu(x):
    return jax.nn.silu(x)

def _sigmoid(x):
    return jax.nn.sigmoid(x)

def _layernorm(x, axis=-1, eps=1e-05):
    m = jnp.mean(x, axis=axis, keepdims=True)
    v = jnp.var(x, axis=axis, keepdims=True)
    return (x - m) / jnp.sqrt(v + eps)

def _scatter_add(tgt, idx, src, axis=0):
    return tgt.at[idx].add(src)

def _segment_sum(src, seg, n):
    return jax.ops.segment_sum(src, seg, n)
kernel_name = 'mk_seq_postln_d1_jaxref_r4_7f0c36'

def setup_inputs(seed: int=0):
    np.random.seed(seed)
    _w = jnp.asarray

    def _L0_attn_setup():
        import jax, jax.numpy as jnp
        import numpy as np
        D_MODEL = 256
        D_HEAD = 64
        N_HEADS = 16
        STATE = 64
        D_INNER = D_HEAD * N_HEADS
        B, T = (4, 512)
        LN_EPS = 1e-05

        def _linear_params(key, fan_out, fan_in):
            k1, k2 = jax.random.split(key)
            s = 1.0 / np.sqrt(fan_in)
            W = jax.random.uniform(k1, (fan_out, fan_in), jnp.float32, -s, s)
            b = jax.random.uniform(k2, (fan_out,), jnp.float32, -s, s)
            return (W, b)

        def _layer_norm(x, gamma, beta):
            mu = jnp.mean(x, axis=-1, keepdims=True)
            var = jnp.mean(jnp.square(x - mu), axis=-1, keepdims=True)
            return (x - mu) * jax.lax.rsqrt(var + LN_EPS) * gamma + beta
        key = jax.random.key(seed)
        ks = jax.random.split(key, 8)
        WQ, bQ = _linear_params(ks[0], D_INNER, D_MODEL)
        WK, bK = _linear_params(ks[1], D_INNER, D_MODEL)
        WV, bV = _linear_params(ks[2], D_INNER, D_MODEL)
        WO, bO = _linear_params(ks[3], D_MODEL, D_INNER)
        Wg, bg = _linear_params(ks[4], D_INNER, D_MODEL)
        alpha_logit = jax.random.normal(ks[5], (N_HEADS, STATE), jnp.float32) * 0.1
        ln_gamma = jnp.ones((D_MODEL,), jnp.float32)
        ln_beta = jnp.zeros((D_MODEL,), jnp.float32)
        x = jax.random.normal(ks[6], (B, T, D_MODEL), jnp.float32)
        return {'x': x, 'WQ': WQ, 'bQ': bQ, 'WK': WK, 'bK': bK, 'WV': WV, 'bV': bV, 'WO': WO, 'bO': bO, 'Wg': Wg, 'bg': bg, 'alpha_logit': alpha_logit, 'ln_gamma': ln_gamma, 'ln_beta': ln_beta}
    _L0_attn_in = _L0_attn_setup()

    def _L0_ffn_setup():
        import jax, jax.numpy as jnp
        import numpy as np
        B, S, DIM = (4, 1024, 256)
        BASE_COUPLING = 0.1
        NUM_CYCLES = 3

        def _gelu(x):
            return jax.nn.gelu(x, approximate=False)

        def _coupling_net(h, w1, b1, w2, b2, w3, b3, w4, b4):
            h = _gelu(h @ w1 + b1)
            h = _gelu(h @ w2 + b2)
            h = _gelu(h @ w3 + b3)
            return jax.nn.sigmoid(h @ w4 + b4)

        def _global_net(h, w1, b1, w2, b2, w3, b3):
            h = _gelu(h @ w1 + b1)
            h = _gelu(h @ w2 + b2)
            return jax.nn.sigmoid(h @ w3 + b3)

        def _twist(x):
            o_r, o_i, p_r, p_i = jnp.split(x, 4, axis=-1)
            return jnp.concatenate([p_r, -p_i, -o_r, o_i], axis=-1)
        key = jax.random.key(seed)
        ks = jax.random.split(key, 9)
        d = DIM

        def w(k, fan_in, fan_out):
            return jax.random.normal(k, (fan_in, fan_out), dtype=jnp.float32) / np.sqrt(fan_in).astype(np.float32)
        inp = {'x': jax.random.normal(ks[0], (B, S, d), dtype=jnp.float32)}
        cn_dims = [(d, d), (d, d // 2), (d // 2, d // 4), (d // 4, 1)]
        for i, (a, b) in enumerate(cn_dims):
            inp[f'cn_w{i + 1}'] = w(ks[1 + i], a, b)
            inp[f'cn_b{i + 1}'] = jnp.zeros((b,), dtype=jnp.float32)
        gc_dims = [(d, d // 2), (d // 2, d // 4), (d // 4, 1)]
        for i, (a, b) in enumerate(gc_dims):
            inp[f'gc_w{i + 1}'] = w(ks[5 + i], a, b)
            inp[f'gc_b{i + 1}'] = jnp.zeros((b,), dtype=jnp.float32)
        inp['adaptive_range'] = jnp.full((1,), 0.2, dtype=jnp.float32)
        return inp
    _L0_ffn_in = _L0_ffn_setup()
    _d = {'L0_attn_x': _L0_attn_in['x'], 'L0_attn_WQ': _L0_attn_in['WQ'], 'L0_attn_bQ': _L0_attn_in['bQ'], 'L0_attn_WK': _L0_attn_in['WK'], 'L0_attn_bK': _L0_attn_in['bK'], 'L0_attn_WV': _L0_attn_in['WV'], 'L0_attn_bV': _L0_attn_in['bV'], 'L0_attn_WO': _L0_attn_in['WO'], 'L0_attn_bO': _L0_attn_in['bO'], 'L0_attn_Wg': _L0_attn_in['Wg'], 'L0_attn_bg': _L0_attn_in['bg'], 'L0_attn_alpha_logit': _L0_attn_in['alpha_logit'], 'L0_attn_ln_gamma': _L0_attn_in['ln_gamma'], 'L0_attn_ln_beta': _L0_attn_in['ln_beta'], 'L0_ffn_cn_w1': _L0_ffn_in['cn_w1'], 'L0_ffn_cn_b1': _L0_ffn_in['cn_b1'], 'L0_ffn_cn_w2': _L0_ffn_in['cn_w2'], 'L0_ffn_cn_b2': _L0_ffn_in['cn_b2'], 'L0_ffn_cn_w3': _L0_ffn_in['cn_w3'], 'L0_ffn_cn_b3': _L0_ffn_in['cn_b3'], 'L0_ffn_cn_w4': _L0_ffn_in['cn_w4'], 'L0_ffn_cn_b4': _L0_ffn_in['cn_b4'], 'L0_ffn_gc_w1': _L0_ffn_in['gc_w1'], 'L0_ffn_gc_b1': _L0_ffn_in['gc_b1'], 'L0_ffn_gc_w2': _L0_ffn_in['gc_w2'], 'L0_ffn_gc_b2': _L0_ffn_in['gc_b2'], 'L0_ffn_gc_w3': _L0_ffn_in['gc_w3'], 'L0_ffn_gc_b3': _L0_ffn_in['gc_b3'], 'L0_ffn_adaptive_range': _L0_ffn_in['adaptive_range']}
    _x0 = _d['L0_attn_x']
    _d['L0_attn_x'] = jax.random.normal(jax.random.fold_in(jax.random.key(seed), 1), (4, 2048, 256), dtype=_x0.dtype)
    del _x0
    return _d

def reference(L0_attn_x, L0_attn_WQ, L0_attn_bQ, L0_attn_WK, L0_attn_bK, L0_attn_WV, L0_attn_bV, L0_attn_WO, L0_attn_bO, L0_attn_Wg, L0_attn_bg, L0_attn_alpha_logit, L0_attn_ln_gamma, L0_attn_ln_beta, L0_ffn_cn_w1, L0_ffn_cn_b1, L0_ffn_cn_w2, L0_ffn_cn_b2, L0_ffn_cn_w3, L0_ffn_cn_b3, L0_ffn_cn_w4, L0_ffn_cn_b4, L0_ffn_gc_w1, L0_ffn_gc_b1, L0_ffn_gc_w2, L0_ffn_gc_b2, L0_ffn_gc_w3, L0_ffn_gc_b3, L0_ffn_adaptive_range):

    def _L0_attn_ref(x, WQ, bQ, WK, bK, WV, bV, WO, bO, Wg, bg, alpha_logit, ln_gamma, ln_beta):
        import jax, jax.numpy as jnp
        import numpy as np
        D_MODEL = 256
        D_HEAD = 64
        N_HEADS = 16
        STATE = 64
        D_INNER = D_HEAD * N_HEADS
        B, T = (4, 512)
        LN_EPS = 1e-05

        def _linear_params(key, fan_out, fan_in):
            k1, k2 = jax.random.split(key)
            s = 1.0 / np.sqrt(fan_in)
            W = jax.random.uniform(k1, (fan_out, fan_in), jnp.float32, -s, s)
            b = jax.random.uniform(k2, (fan_out,), jnp.float32, -s, s)
            return (W, b)

        def _layer_norm(x, gamma, beta):
            mu = jnp.mean(x, axis=-1, keepdims=True)
            var = jnp.mean(jnp.square(x - mu), axis=-1, keepdims=True)
            return (x - mu) * jax.lax.rsqrt(var + LN_EPS) * gamma + beta
        batch, seq_len, _ = x.shape
        residual = x
        xn = _layer_norm(x, ln_gamma, ln_beta)
        Q = (xn @ WQ.T + bQ).reshape(batch, seq_len, N_HEADS, D_HEAD)
        K = (xn @ WK.T + bK).reshape(batch, seq_len, N_HEADS, D_HEAD)
        V = (xn @ WV.T + bV).reshape(batch, seq_len, N_HEADS, D_HEAD)
        gate = jax.nn.silu(xn @ Wg.T + bg).reshape(batch, seq_len, N_HEADS, D_HEAD)
        alpha = jax.nn.sigmoid(alpha_logit)
        Qs = Q[..., :STATE]
        Ks = K[..., :STATE]

        def step(h, qkv):
            q, k, v = qkv
            h = alpha[None, :, :, None] * h + k[:, :, :, None] * v[:, :, None, :]
            o = jnp.einsum('bhi,bhij->bhj', q, h)
            return (h, o)
        h0 = jnp.zeros((batch, N_HEADS, STATE, D_HEAD), x.dtype)
        qkv_t = (jnp.moveaxis(Qs, 1, 0), jnp.moveaxis(Ks, 1, 0), jnp.moveaxis(V, 1, 0))
        _, o = jax.lax.scan(step, h0, qkv_t)
        o = jnp.moveaxis(o, 0, 1)
        o = o * gate
        y = o.reshape(batch, seq_len, D_INNER) @ WO.T + bO
        return residual + y

    def _L0_ffn_ref(x, cn_w1, cn_b1, cn_w2, cn_b2, cn_w3, cn_b3, cn_w4, cn_b4, gc_w1, gc_b1, gc_w2, gc_b2, gc_w3, gc_b3, adaptive_range):
        import jax, jax.numpy as jnp
        import numpy as np
        B, S, DIM = (4, 1024, 256)
        BASE_COUPLING = 0.1
        NUM_CYCLES = 3

        def _gelu(x):
            return jax.nn.gelu(x, approximate=False)

        def _coupling_net(h, w1, b1, w2, b2, w3, b3, w4, b4):
            h = _gelu(h @ w1 + b1)
            h = _gelu(h @ w2 + b2)
            h = _gelu(h @ w3 + b3)
            return jax.nn.sigmoid(h @ w4 + b4)

        def _global_net(h, w1, b1, w2, b2, w3, b3):
            h = _gelu(h @ w1 + b1)
            h = _gelu(h @ w2 + b2)
            return jax.nn.sigmoid(h @ w3 + b3)

        def _twist(x):
            o_r, o_i, p_r, p_i = jnp.split(x, 4, axis=-1)
            return jnp.concatenate([p_r, -p_i, -o_r, o_i], axis=-1)
        global_context = x.mean(axis=1, keepdims=True)
        gf = _global_net(global_context, gc_w1, gc_b1, gc_w2, gc_b2, gc_w3, gc_b3)
        out = x
        for _ in range(NUM_CYCLES):
            tf = _coupling_net(out, cn_w1, cn_b1, cn_w2, cn_b2, cn_w3, cn_b3, cn_w4, cn_b4)
            combined = 0.7 * gf + 0.3 * tf
            coupling = BASE_COUPLING + adaptive_range * (combined - 0.5) * 2.0
            out = out + coupling * _twist(out)
        return out
    x = L0_attn_x
    x = _layernorm(x + _L0_attn_ref(x, L0_attn_WQ, L0_attn_bQ, L0_attn_WK, L0_attn_bK, L0_attn_WV, L0_attn_bV, L0_attn_WO, L0_attn_bO, L0_attn_Wg, L0_attn_bg, L0_attn_alpha_logit, L0_attn_ln_gamma, L0_attn_ln_beta), axis=-1)
    x = _layernorm(x + _L0_ffn_ref(x, L0_ffn_cn_w1, L0_ffn_cn_b1, L0_ffn_cn_w2, L0_ffn_cn_b2, L0_ffn_cn_w3, L0_ffn_cn_b3, L0_ffn_cn_w4, L0_ffn_cn_b4, L0_ffn_gc_w1, L0_ffn_gc_b1, L0_ffn_gc_w2, L0_ffn_gc_b2, L0_ffn_gc_w3, L0_ffn_gc_b3, L0_ffn_adaptive_range), axis=-1)
    return x

_drawn_inputs = setup_inputs


def setup_inputs(seed=0):
    import zlib

    import numpy as np

    out = dict(_drawn_inputs(seed))
    spreads = {'L0_attn_ln_gamma': (1.0, 0.2),
     'L0_attn_ln_beta': (0.0, 0.1),
     'L0_ffn_cn_b1': (0.0, 2.0),
     'L0_ffn_cn_b2': (0.0, 2.0),
     'L0_ffn_cn_b3': (0.0, 2.0),
     'L0_ffn_gc_b1': (0.0, 2.0),
     'L0_ffn_gc_b2': (0.0, 2.0)}
    factors = {'L0_attn_bQ': 5.082,
     'L0_attn_bK': 4.878,
     'L0_attn_bV': 4.818,
     'L0_attn_bO': 6.275,
     'L0_attn_bg': 4.956,
     'L0_attn_alpha_logit': 7.754,
     'L0_ffn_cn_w1': 7.425,
     'L0_ffn_cn_w2': 7.705,
     'L0_ffn_cn_w3': 6.187,
     'L0_ffn_cn_w4': 6.996,
     'L0_ffn_gc_w1': 64.0,
     'L0_ffn_gc_w2': 8.0,
     'L0_ffn_gc_w3': 6.074}
    for name, (base, spread) in spreads.items():
        noise = np.random.default_rng([zlib.crc32(name.encode()), seed]).standard_normal(out[name].shape)
        drawn = base * np.exp(spread * noise) if base else spread * noise
        out[name] = jnp.asarray(drawn.astype(out[name].dtype))
    for name, factor in factors.items():
        out[name] = (out[name] * factor).astype(out[name].dtype)
    return out
```

```python
from contextlib import ExitStack

import concourse.bass as bass
from concourse import mybir

f32 = mybir.dt.float32
f32r = mybir.dt.float32r
i32 = mybir.dt.int32
ALU = mybir.AluOpType
ACT = mybir.ActivationFunctionType
AX = mybir.AxisListType

B, T, D = 4, 2048, 256
NH, DH = 16, 64
DI = NH * DH
P = 128
KT = D // P
NP = NH // 2
ST = 512
NS = T // ST
C = 128
NC = ST // C
BL = 32
NB = C // BL
MID = BL // 2
EPS = 1e-5
CYCLES = 3
GT = 2
NG = NS // GT
VIS = CYCLES * NG


def build(nc, a, out):
    ctx = ExitStack()
    with ctx:
        def sb(name, shape, dt=f32):
            return ctx.enter_context(nc.sbuf_tensor(name, shape, dt))

        def sem(name):
            return ctx.enter_context(nc.semaphore(name))

        w_hi = {n: sb(f"w{n}_hi", [P, KT, DI], f32r) for n in "qkvg"}
        w_lo = {n: sb(f"w{n}_lo", [P, KT, DI], f32r) for n in "qkvg"}
        wo = sb("wo", [P, NP, D])
        ident = sb("ident", [P, P])
        causal = sb("causal", [P, P])
        col_bias = sb("col_bias", [P, 3, NP])
        bias_v = sb("bias_v", [P, DI])
        bias_o = sb("bias_o", [P, D])
        gamma = sb("gamma", [P, KT])
        beta = sb("beta", [P, KT])
        NPOW = C + BL + C + 2
        logit = sb("logit", [P, NP])
        grown = sb("grown", [P, 8, NP])
        shrunk = sb("shrunk", [P, 5, NP])
        pows = sb("pows", [P, NP, NPOW])
        half_neg = sb("half_neg", [P, NC])
        f_w1 = sb("f_w1", [P, KT, D])
        f_w2 = sb("f_w2", [P, KT, P])
        f_w3 = sb("f_w3", [P, DH])
        f_w4 = sb("f_w4", [P, P])
        g_w1 = sb("g_w1", [P, KT, P])
        g_w2 = sb("g_w2", [P, DH])
        g_w3 = sb("g_w3", [DH, P])
        f_b1 = sb("f_b1", [P, KT])
        f_b2 = sb("f_b2", [P, 1])
        f_b3 = sb("f_b3", [P, 1])
        f_b4 = sb("f_b4", [P, 1])
        g_b1 = sb("g_b1", [P, 1])
        g_b2 = sb("g_b2", [DH, 1])
        g_b3 = sb("g_b3", [P, 1])
        w4c = sb("w4c", [P, 1])
        gw3c = sb("gw3c", [DH, 1])
        rng = sb("rng", [P, 1])
        rng3 = sb("rng3", [P, 1])
        rng7 = sb("rng7", [P, 1])
        sign = sb("sign", [P, KT])
        x_in = sb("x_in", [P, NC, D])
        x_nf = sb("x_nf", [P, 2, KT * ST])
        x_n = x_nf[:, 0, :].rearrange("p (c d) -> p c d", c=NC)
        x_f = x_nf[:, 1, :].rearrange("p (k n) -> p k n", k=KT)
        x_2b = sb("x_2b", [P, NC, D])
        stats = sb("stats", [P, NC, 6])
        mv = sb("mv", [P, NC, 2])
        vare = sb("vare", [P, NC])
        rstd = sb("rstd", [P, NC])
        x_hi = sb("x_hi", [P, KT, ST], f32r)
        x_lo = sb("x_lo", [P, KT, ST], f32r)
        v_sb = sb("v_sb", [P, NC, DI])
        q_sb = sb("q_sb", [P, NB, NC, C])
        k_sc = sb("k_sc", [P, NC, C])
        k_end = sb("k_end", [P, NC, C])
        k_tok = sb("k_tok", [P, NC, C])
        att = sb("att", [P, 2, NC, C])
        gate = sb("gate", [P, ST])
        h_seq = sb("h_seq", [P, NP, NC + 1, DH])
        h_bd = sb("h_bd", [P, NC, P])
        o_g = sb("o_g", [P, NP, ST])
        x1t = sb("x1t", [P, KT, T])
        msum = sb("msum", [P, KT])
        gf1 = sb("gf1", [P, 1])
        gf2 = sb("gf2", [DH, 1])
        gf3 = sb("gf3", [P, 1])
        base = sb("base", [P, 1])
        out_t = v_sb[:].rearrange("p (k c) n -> p k (c n)", k=KT)
        h1 = o_g[:].rearrange("p (t m) n -> p t m n", m=2)
        h2 = x_nf[:].rearrange("p a (t n) -> p (a t) n", n=ST)
        h3 = x_2b[:].rearrange("p (g c) d -> p g (c d)", g=NG)
        th = k_sc[:].rearrange("p c n -> p (c n)")
        cpl = k_end[:].rearrange("p c n -> p (c n)")
        turned = q_sb[:].rearrange("p b c n -> p (b c n)")[:, 0:KT * ST].rearrange("p (k n) -> p k n", k=KT)
        fin = q_sb[:].rearrange("p b c n -> p (b c n)")[:, KT * ST:2 * KT * ST].rearrange("p (c n) -> p c n", c=NC)
        w_in = out_t[:, :, 0:DI]

        bank = [ctx.enter_context(nc.psum_tensor(f"bank{n}", [P, ST], f32)) for n in range(8)]

        def part(n, k):
            return bank[n][:].rearrange("p (c n) -> p c n", c=k)

        s_const = sem("small_constants_loaded")
        s_wo = sem("wo_loaded")
        s_wdma = sem("weight_arrived")
        s_whi = sem("weight_hi_made")
        s_wlo = sem("weight_lo_made")
        s_setp = sem("pool_setup")
        s_setv = sem("vector_setup")
        s_alpha = sem("alpha_done")
        s_pow = sem("power_step")
        s_x = sem("x_loaded")
        s_xfree = sem("x_in_read")
        s_st = sem("stats_step")
        s_stats = sem("x_stats_ready")
        s_rstd = sem("x_rstd_ready")
        s_x2b = sem("x_2b_ready")
        s_xn = sem("x_n_ready")
        s_xt = sem("x_transposed")
        s_xf = sem("x_f_ready")
        s_xhi = sem("x_hi_ready")
        s_xlo = sem("x_lo_ready")
        s_proj = sem("projection_ready")
        s_vev = sem("v_evacuated")
        s_kev = sem("k_evacuated")
        s_qev = sem("q_evacuated")
        s_gev = sem("gate_evacuated")
        s_kt = sem("k_end_transposed")
        s_ktok = sem("k_tok_ready")
        s_score = sem("scores_ready")
        s_att = sem("scores_masked")
        s_upd = sem("state_update_ready")
        s_h0 = sem("state_rows_cleared")
        s_hs = sem("state_step")
        s_hbd = sem("state_diagonal_ready")
        s_o = sem("o_ready")
        s_og = sem("o_gated")
        s_y = sem("y_ready")
        s_r = sem("residual_sum_ready")
        s_r1 = sem("ln1_stats_ready")
        s_rs1 = sem("ln1_rstd_ready")
        s_x1 = sem("x1_ready")
        s_x1t = sem("x1_transposed")
        s_x1c = sem("x1t_copied")
        s_ms = sem("mean_ready")
        s_gp = sem("global_net_product")
        s_ga = sem("global_net_activation")
        s_base = sem("base_ready")
        s_l1 = sem("layer1_ready")
        s_h1 = sem("h1_ready")
        s_l2 = sem("layer2_ready")
        s_h2 = sem("h2_ready")
        s_l3 = sem("layer3_ready")
        s_h3 = sem("h3_ready")
        s_l4 = sem("layer4_ready")
        s_th = sem("tanh_ready")
        s_cpl = sem("coupling_ready")
        s_tu = sem("turned_ready")
        s_up = sem("out_updated")
        s_y2 = sem("final_sum_ready")
        s_yt = sem("final_transposed")
        s_st2 = sem("ln2_stats_ready")
        s_rs2 = sem("ln2_rstd_ready")
        s_fin = sem("final_rows_ready")
        s_out = sem("out_stored")
        s_passed = sem("vector_passed")
        s_passed_pe = sem("tensor_passed")

        C0 = 1
        started = [s_xfree, s_r, s_proj, s_xlo, s_og, s_upd, s_o, s_x1t, s_att, s_fin, s_ktok, s_hs, s_hbd,
                   s_score, s_kt, s_x1c, s_out]

        block = ctx.enter_context(nc.Block())

        consts = [
            (col_bias[:, 0, :], a["bQ"]),
            (col_bias[:, 1, :], a["bK"]),
            (col_bias[:, 2, :], a["bg"]),
            (bias_v[:], a["bV"].unsqueeze(0).broadcast_to([P, DI])),
            (bias_o[:], a["bO"].unsqueeze(0).broadcast_to([P, D])),
            (gamma[:], a["gamma"]),
            (beta[:], a["beta"]),
            (f_w1[:], a["cn_w1"].rearrange("(k p) n -> p k n", p=P)),
            (f_w2[:], a["cn_w2"].rearrange("(k p) n -> p k n", p=P)),
            (f_w3[:], a["cn_w3"]),
            (w4c[0:DH, :], a["cn_w4"]),
            (w4c[DH:P, :], a["cn_w4"]),
            (g_w1[:], a["gc_w1"].rearrange("(k p) n -> p k n", p=P)),
            (g_w2[:], a["gc_w2"]),
            (gw3c[:], a["gc_w3"]),
            (f_b1[:], a["cn_b1"]),
            (f_b2[:], a["cn_b2"]),
            (f_b3[0:DH, :], a["cn_b3"].rearrange("(p n) -> p n", n=1)),
            (f_b3[DH:P, :], a["cn_b3"].rearrange("(p n) -> p n", n=1)),
            (f_b4[:], a["cn_b4"].unsqueeze(0).broadcast_to([P, 1])),
            (g_b1[:], a["gc_b1"].rearrange("(p n) -> p n", n=1)),
            (g_b2[:], a["gc_b2"].rearrange("(p n) -> p n", n=1)),
            (g_b3[:], a["gc_b3"].unsqueeze(0).broadcast_to([P, 1])),
            (rng[:], a["range"].unsqueeze(0).broadcast_to([P, 1])),
        ]
        x_rows = a["x"].rearrange("(i c p) d -> i p c d", c=NC, p=P)
        out_rows = out.rearrange("(i c p) d -> i p c d", c=NC, p=P)

        QP, KP, EP, HP = 0, C, C + BL, C + BL + C

        @block.sync
        def _(sp):
            for counter in started:
                sp.sem_inc(counter, C0)
            sp.dma_start(logit[:], a["alpha"]).then_inc(s_alpha, 16)
            for n, w in enumerate("qkvg"):
                if n:
                    sp.wait_ge(s_wlo, n)
                sp.dma_start(w_in, a["w" + w].rearrange("(k p) n -> p k n", p=P)).then_inc(s_wdma, 16)
            sp.dma_start(wo[:], a["wo"].rearrange("(n p) m -> p n m", p=P)).then_inc(s_wo, 16)
            with sp.Fori(0, B) as b:
                with sp.Fori(0, NS) as s:
                    it = b * NS + s
                    sp.wait_ge(s_xfree, it * 2 + C0)
                    sp.dma_start(x_in[:], x_rows[it]).then_inc(s_x, 16)
                for t in range(NS):
                    sp.wait_ge(s_fin, b * NS + t + 1 + C0)
                    sp.dma_start(out_rows[b * NS + t], fin).then_inc(s_out, 16)
            sp.wait_ge(s_out, 16 * B * NS + C0)

        @block.gpsimd
        def _(pool):
            for dst, src in consts:
                pool.dma_start(dst, src).then_inc(s_const, 16)
            nc.gpsimd.memset(ident[:], 0.0).then_inc(s_setp, 1)
            nc.gpsimd.memset(causal[:], 1.0).then_inc(s_setp, 1)
            nc.gpsimd.memset(half_neg[:], -0.5).then_inc(s_setp, 1)
            pool.wait_ge(s_setp, 3)
            nc.gpsimd.affine_select(out=ident[:], in_=ident[:], compare_op=ALU.not_equal, fill=1.0,
                                    base=0, pattern=[[-1, P]], channel_multiplier=1).then_inc(s_setp, 1)
            nc.gpsimd.affine_select(out=causal[:], in_=causal[:], compare_op=ALU.is_ge, fill=0.0,
                                    base=0, pattern=[[1, P]], channel_multiplier=-1).then_inc(s_setp, 1)
            pool.wait_ge(s_const, 16 * len(consts))
            with pool.Fori(0, B) as b:
                with pool.Fori(0, NS) as s:
                    it = b * NS + s
                    pool.wait_ge(s_x, (it + 1) * 16)
                    pool.wait_ge(s_r, it * 2 + C0)
                    nc.gpsimd.tensor_tensor(x_2b[:], x_in[:], bias_o[:].unsqueeze(1).broadcast_to([P, NC, D]),
                                            ALU.add).then_inc(s_x2b, 1)
                    pool.wait_ge(s_x2b, it * 2 + 1)
                    nc.gpsimd.tensor_tensor(x_2b[:], x_2b[:], x_in[:], ALU.add).then_inc(s_x2b, 1)
                    pool.wait_ge(s_x2b, it * 2 + 2)
                    pool.sem_inc(s_xfree, 1)
                    pool.wait_ge(s_stats, it + 1)
                    nc.gpsimd.tensor_tensor(rstd[:], vare[:], half_neg[:], ALU.pow).then_inc(s_rstd, 1)
                    pool.wait_ge(s_r1, it + 1)
                    nc.gpsimd.tensor_tensor(rstd[:], vare[:], half_neg[:], ALU.pow).then_inc(s_rs1, 1)
                for t in range(NS):
                    pool.wait_ge(s_st2, b * NS + t + 1)
                    nc.gpsimd.tensor_tensor(rstd[:], vare[:], half_neg[:], ALU.pow).then_inc(s_rs2, 1)

        order = []
        for r in range(CYCLES):
            g0, g1 = NG * r, NG * r + 1
            order += [(1, g0)] + ([(3, g0 - 1), (4, g0 - 1)] if r else [])
            order += [(2, g0), (3, g0), (1, g1), (4, g0), (2, g1)]
        order += [(3, VIS - 1), (4, VIS - 1)]

        def tile_cols(t):
            return slice(t * ST, (t + 1) * ST)

        @block.scalar
        def _(act):
            act.wait_ge(s_alpha, 16)
            nc.scalar.activation(grown[:, 0, :], logit[:], ACT.Sigmoid).then_inc(s_alpha, 1)
            for n, w in enumerate("qkvg"):
                act.wait_ge(s_wdma, 16 * (n + 1))
                nc.scalar.activation(w_hi[w][:], w_in, ACT.Copy).then_inc(s_whi, 1)
            act.wait_ge(s_const, 16 * len(consts))
            act.wait_ge(s_pow, 36)
            with act.Fori(0, B) as b:
                with act.Fori(0, NS) as s:
                    it = b * NS + s
                    for k in range(KT):
                        act.wait_ge(s_xt, it * KT + k + 1)
                        if k == 0:
                            act.wait_ge(s_proj, it * 32 + C0)
                            act.wait_ge(s_xlo, it + C0)
                        nc.scalar.activation(x_f[:, k, :], bank[2 + k][:], ACT.Identity,
                                             bias=beta[:, k:k + 1], scale=gamma[:, k:k + 1]).then_inc(s_xf, 1)
                    act.wait_ge(s_xf, it * KT + KT)
                    nc.scalar.activation(x_hi[:], x_f, ACT.Copy).then_inc(s_xhi, 1)

                    def gate_of(p):
                        act.wait_ge(s_proj, it * 32 + 8 + 3 * p + 3 + C0)
                        act.wait_ge(s_og, it * NP + p + C0)
                        nc.scalar.activation(gate[:], bank[0 if p % 2 == 0 else 1][:], ACT.Silu,
                                             bias=col_bias[:, 2, p:p + 1]).then_inc(s_gev, 1)

                    for p in range(NP):
                        act.wait_ge(s_kt, it * NP + p + 1 + C0)
                        act.wait_ge(s_upd, it * NP + p + C0)
                        nc.scalar.activation(k_tok[:], part(4, NC), ACT.Copy).then_inc(s_ktok, 1)
                        if p == 0:
                            gate_of(0)
                        act.wait_ge(s_hs, (it * NP + p + 1) * (NC + 1) + C0)
                        act.wait_ge(s_o, it * NP + p + C0)
                        for e in range(2):
                            rows = slice(e * DH, (e + 1) * DH)
                            nc.scalar.activation(h_bd[rows, :, e * DH:(e + 1) * DH], h_seq[rows, p, 0:NC, :],
                                                 ACT.Copy, scale=pows[rows, p, HP:HP + 1]).then_inc(s_hbd, 1)
                        if p + 1 < NP:
                            gate_of(p + 1)
                    for k in range(KT):
                        act.wait_ge(s_x1t, it * KT + k + 1 + C0)
                        nc.scalar.activation(x1t[:, k, bass.ds(s * ST, ST)], bank[7 if k == 0 else 4][:],
                                             ACT.Copy).then_inc(s_x1c, 1)
                act.wait_ge(s_gp, b * 3 + 1)
                nc.scalar.activation(gf1[:], bank[7][:, 0:1], ACT.Gelu, bias=g_b1[:], scale=1.0 / T).then_inc(s_ga, 1)
                act.wait_ge(s_gp, b * 3 + 2)
                nc.scalar.activation(gf2[:], bank[7][0:DH, 1:2], ACT.Gelu, bias=g_b2[:]).then_inc(s_ga, 1)
                act.wait_ge(s_gp, b * 3 + 3)
                nc.scalar.activation(gf3[:], bank[7][:, 2:3], ACT.Tanh, bias=g_b3[:], scale=0.5).then_inc(s_ga, 1)
                for layer, n in order:
                    g = n % NG
                    v = b * VIS + n
                    if layer == 1:
                        for j in range(GT):
                            for m in range(2):
                                act.wait_ge(s_l1, v * 4 + 2 * j + m + 1)
                                if n >= NG:
                                    act.wait_ge(s_l2, (v - NG) * GT + j + 1)
                                nc.scalar.activation(h1[:, g * GT + j, m, :], bank[2 * j + m][:], ACT.Gelu,
                                                     bias=f_b1[:, m:m + 1]).then_inc(s_h1, 1)
                    if layer == 2:
                        for j in range(GT):
                            act.wait_ge(s_l2, v * GT + j + 1)
                            if n >= NG:
                                act.wait_ge(s_l3, v - NG + 1)
                            nc.scalar.activation(h2[:, g * GT + j, :], bank[4 + j][:], ACT.Gelu,
                                                 bias=f_b2[:]).then_inc(s_h2, 1)
                    if layer == 3:
                        act.wait_ge(s_l3, v + 1)
                        if n >= NG:
                            act.wait_ge(s_l4, (v - NG) * GT + GT)
                        nc.scalar.activation(h3[:, g, :], bank[6][:], ACT.Gelu, bias=f_b3[:]).then_inc(s_h3, 1)
                    if layer == 4:
                        for j in range(GT):
                            act.wait_ge(s_l4, v * GT + j + 1)
                            if n or j:
                                act.wait_ge(s_cpl, v * GT + j)
                            nc.scalar.activation(th, bank[7][:], ACT.Tanh, bias=f_b4[:],
                                                 scale=0.5).then_inc(s_th, 1)

        @block.vector
        def _(dve):
            nc.vector.memset(att[:].bitcast(i32), 0).then_inc(s_setv, 1)
            nc.vector.memset(h_bd[:].bitcast(i32), 0).then_inc(s_setv, 1)
            nc.vector.memset(bank[2][:], 0.0).then_inc(s_setv, 1)
            nc.vector.memset(bank[3][:], 0.0).then_inc(s_setv, 1)
            nc.vector.memset(sign[:], 1.0).then_inc(s_setv, 1)
            nc.vector.memset(f_w4[:], 1.0).then_inc(s_setv, 1)
            nc.vector.memset(g_w3[:], 1.0).then_inc(s_setv, 1)
            dve.wait_ge(s_setv, 7)
            nc.vector.memset(sign[DH:P, 0:1], -1.0).then_inc(s_setv, 1)
            nc.vector.memset(sign[0:DH, 1:2], -1.0).then_inc(s_setv, 1)
            dve.wait_ge(s_const, 16 * len(consts))
            nc.vector.tensor_scalar(f_w4[:], f_w4[:], w4c[:], None, ALU.mult).then_inc(s_setv, 1)
            nc.vector.tensor_scalar(g_w3[:], g_w3[:], gw3c[:], None, ALU.mult).then_inc(s_setv, 1)
            nc.vector.tensor_scalar(rng3[:], rng[:], 0.3, None, ALU.mult).then_inc(s_setv, 1)
            nc.vector.tensor_scalar(rng7[:], rng[:], 0.7, None, ALU.mult).then_inc(s_setv, 1)
            nc.vector.tensor_scalar(f_b4[:], f_b4[:], 0.5, None, ALU.mult).then_inc(s_setv, 1)
            nc.vector.tensor_scalar(g_b3[:], g_b3[:], 0.5, None, ALU.mult).then_inc(s_setv, 1)
            steps = [0]

            def link(ins):
                steps[0] += 1
                ins.then_inc(s_pow, 1)
                dve.wait_ge(s_pow, steps[0])

            dve.wait_ge(s_alpha, 17)
            link(nc.vector.reciprocal(shrunk[:, 0, :], grown[:, 0, :]))
            for n in range(7):
                link(nc.vector.tensor_tensor(grown[:, n + 1, :], grown[:, n, :], grown[:, n, :], ALU.mult))
            for n in range(4):
                link(nc.vector.tensor_tensor(shrunk[:, n + 1, :], shrunk[:, n, :], shrunk[:, n, :], ALU.mult))

            def times(dst, src, w):
                by = grown[:, w, :].unsqueeze(2).broadcast_to([P, NP, 1 << w])
                width = dst.shape[-1]
                link(nc.vector.tensor_tensor(dst, src, by[:, :, 0:width], ALU.mult))

            link(nc.vector.tensor_copy(pows[:, :, QP:QP + 1], shrunk[:, 4, :].unsqueeze(2)))
            for w in range(7):
                n = 1 << w
                times(pows[:, :, QP + n:QP + 2 * n], pows[:, :, QP:QP + n], w)
            link(nc.vector.tensor_copy(pows[:, :, KP + BL - 1:KP + BL], pows[:, :, QP + 1:QP + 2]))
            link(nc.vector.memset(pows[:, :, EP + C - 1:EP + C], 1.0))
            for w in range(5):
                n, end = 1 << w, KP + BL
                times(pows[:, :, end - 2 * n:end - n], pows[:, :, end - n:end], w)
            for w in range(7):
                n, end = 1 << w, EP + C
                times(pows[:, :, end - 2 * n:end - n], pows[:, :, end - n:end], w)
            link(nc.vector.tensor_copy(pows[:, :, HP:HP + 1], pows[:, :, QP + 2 * MID + 1:QP + 2 * MID + 2]))
            link(nc.vector.tensor_copy(pows[:, :, HP + 1:HP + 2], grown[:, 7, :].unsqueeze(2)))
            for n, w in enumerate("qkvg"):
                dve.wait_ge(s_whi, n + 1)
                nc.vector.tensor_tensor(w_lo[w][:], w_in, w_hi[w][:].bitcast(f32), ALU.subtract).then_inc(s_wlo, 1)
            dve.wait_ge(s_setv, 15)
            dve.wait_ge(s_setp, 5)

            def norm_stats(src, count, done):
                for c in range(NC):
                    nc.vector.bn_stats(stats[:, c, :], src(c)).then_inc(s_st, 1)
                dve.wait_ge(s_st, count + NC)
                dve.sem_inc(s_passed, 1)
                for c in range(NC):
                    nc.vector.bn_aggr(mv[:, c, :], stats[:, c, :]).then_inc(s_st, 1)
                dve.wait_ge(s_st, count + 2 * NC)
                nc.vector.tensor_scalar(vare[:], mv[:, :, 1], EPS, None, ALU.add).then_inc(done, 1)

            def norm_apply(dst, src, done):
                for c in range(NC):
                    last = nc.vector.tensor_scalar(dst(c), src(c), mv[:, c, 0:1], rstd[:, c:c + 1],
                                                   ALU.subtract, ALU.mult)
                last.then_inc(done, 1)

            STC = 4 * NC * NS + 2 * NC * NS
            with dve.Fori(0, B) as b:
                nc.vector.memset(h_seq[:, :, NC, :], 0.0).then_inc(s_h0, 1)
                dve.wait_ge(s_h0, b + 1)
                dve.sem_inc(s_passed, 1)
                with dve.Fori(0, NS) as s:
                    it = b * NS + s
                    dve.wait_ge(s_x, (it + 1) * 16)
                    norm_stats(lambda c: x_in[:, c, :], b * STC + s * 4 * NC, s_stats)
                    dve.wait_ge(s_rstd, it + 1)
                    dve.wait_ge(s_x1t, it * KT + C0)
                    norm_apply(lambda c: x_n[:, c, :], lambda c: x_in[:, c, :], s_xn)
                    dve.wait_ge(s_xn, it + 1)
                    dve.sem_inc(s_xfree, 1)
                    dve.wait_ge(s_xhi, it + 1)
                    dve.wait_ge(s_proj, it * 32 + C0)
                    nc.vector.tensor_tensor(x_lo[:], x_f, x_hi[:].bitcast(f32), ALU.subtract).then_inc(s_xlo, 1)
                    for n in range(2 * NC):
                        c, half = n // 2, n % 2
                        dve.wait_ge(s_proj, it * 32 + n + 1 + C0)
                        cols = slice(half * ST, (half + 1) * ST)
                        nc.vector.tensor_tensor(v_sb[:, c, cols], bank[n % 2][:], bias_v[:, cols],
                                                ALU.add).then_inc(s_vev, 1)

                    def keys_of(p):
                        src = part((3 * p) % 2, NC)
                        dve.wait_ge(s_proj, it * 32 + 8 + 3 * p + 1 + C0)
                        dve.wait_ge(s_score, (it * NP + p) * 2 + C0)
                        nc.vector.scalar_tensor_tensor(
                            k_sc[:].rearrange("p c (b r) -> p (c b) r", r=BL),
                            bank[(3 * p) % 2][:].rearrange("p (c r) -> p c r", r=BL), col_bias[:, 1, p:p + 1],
                            pows[:, p, KP:KP + BL].unsqueeze(1).broadcast_to([P, NC * NB, BL]),
                            ALU.add, ALU.mult)
                        dve.wait_ge(s_kt, it * NP + p + C0)
                        nc.vector.scalar_tensor_tensor(
                            k_end[:], src, col_bias[:, 1, p:p + 1],
                            pows[:, p, EP:EP + C].unsqueeze(1).broadcast_to([P, NC, C]),
                            ALU.add, ALU.mult).then_inc(s_kev, 1)

                    def queries_of(p):
                        src = part((3 * p + 1) % 2, NC)
                        dve.wait_ge(s_proj, it * 32 + 8 + 3 * p + 2 + C0)
                        dve.wait_ge(s_o, it * NP + p + C0)
                        for j in range(NB):
                            last = nc.vector.scalar_tensor_tensor(
                                q_sb[:, j, :, j * BL:C], src[:, :, j * BL:C], col_bias[:, 0, p:p + 1],
                                pows[:, p, QP:QP + C - j * BL].unsqueeze(1).broadcast_to([P, NC, C - j * BL]),
                                ALU.add, ALU.mult)
                        last.then_inc(s_qev, 1)

                    keys_of(0)
                    for p in range(NP):
                        n = it * NP + p
                        if p == 0:
                            queries_of(0)
                        for e in range(2):
                            dve.wait_ge(s_score, n * 2 + e + 1 + C0)
                            if e == 0:
                                dve.wait_ge(s_o, n + C0)
                            dve.sem_inc(s_passed, 1)
                            nc.vector.copy_predicated(
                                att[:, e], causal[:].bitcast(i32).unsqueeze(1).broadcast_to([P, NC, C]),
                                part(2 + e, NC)).then_inc(s_att, 1)
                        dve.wait_ge(s_hbd, n * 2 + C0)
                        nc.vector.tensor_copy(h_seq[:, p, 0, :], h_seq[:, p, NC, :]).then_inc(s_hs, 1)
                        dve.wait_ge(s_upd, n + 1 + C0)
                        for c in range(NC):
                            dve.wait_ge(s_hs, n * (NC + 1) + c + 1 + C0)
                            nc.vector.scalar_tensor_tensor(
                                h_seq[:, p, c + 1, :], h_seq[:, p, c, :], pows[:, p, HP + 1:HP + 2],
                                bank[6][:, c * DH:(c + 1) * DH], ALU.mult, ALU.add).then_inc(s_hs, 1)
                        if p + 1 < NP:
                            keys_of(p + 1)
                        dve.wait_ge(s_o, n + 1 + C0)
                        dve.wait_ge(s_gev, n + 1)
                        nc.vector.tensor_tensor(o_g[:, p, :], bank[5][:], gate[:], ALU.mult).then_inc(s_og, 1)
                        if p + 1 < NP:
                            queries_of(p + 1)
                    for h in range(2):
                        dve.wait_ge(s_y, it * 2 + h + 1)
                        dve.wait_ge(s_x2b, it * 2 + 2)
                        nc.vector.tensor_tensor(x_n[:, 2 * h:2 * h + 2, :], x_2b[:, 2 * h:2 * h + 2, :],
                                                part(h, 2), ALU.add).then_inc(s_r, 1)
                    dve.wait_ge(s_r, it * 2 + 2 + C0)
                    norm_stats(lambda c: x_n[:, c, :], b * STC + s * 4 * NC + 2 * NC, s_r1)
                    dve.wait_ge(s_rs1, it + 1)
                    norm_apply(lambda c: x_n[:, c, :], lambda c: x_n[:, c, :], s_x1)
                dve.wait_ge(s_x1c, (b + 1) * NS * KT + C0)
                nc.vector.tensor_reduce(msum[:], x1t[:], AX.X, ALU.add).then_inc(s_ms, 1)
                dve.wait_ge(s_ga, b * 3 + 3)
                nc.vector.tensor_scalar(base[:], gf3[:], rng7[:], 0.1, ALU.mult, ALU.add).then_inc(s_base, 1)
                dve.wait_ge(s_base, b + 1)
                for n in range(VIS):
                    for j in range(GT):
                        t = (n % NG) * GT + j
                        u = (b * VIS + n) * GT + j
                        src = x1t if n < NG else out_t
                        dve.wait_ge(s_th, u + 1)
                        nc.vector.tensor_scalar(cpl, th, rng3[:], base[:], ALU.mult, ALU.add).then_inc(s_cpl, 1)
                        dve.wait_ge(s_cpl, u + 1)
                        nc.vector.tensor_tensor(turned[:, 0, :], src[:, 1, tile_cols(t)], cpl, ALU.mult)
                        nc.vector.tensor_tensor(turned[:, 1, :], src[:, 0, tile_cols(t)], cpl,
                                                ALU.mult).then_inc(s_tu, 1)
                        dve.wait_ge(s_tu, u + 1)
                        for k in range(KT):
                            last = nc.vector.scalar_tensor_tensor(
                                out_t[:, k, tile_cols(t)], turned[:, k, :], sign[:, k:k + 1],
                                src[:, k, tile_cols(t)], ALU.mult, ALU.add)
                        last.then_inc(s_up, 1)
                        if n >= VIS - NG:
                            dve.wait_ge(s_up, u + 1)
                            nc.vector.tensor_tensor(out_t[:, :, tile_cols(t)], out_t[:, :, tile_cols(t)],
                                                    x1t[:, :, tile_cols(t)], ALU.add).then_inc(s_y2, 1)
                for t in range(NS):
                    pb = 2 * (t % 2)
                    dve.wait_ge(s_yt, b * NS + t + 1)

                    def rows(c, pb=pb):
                        return bank[pb + c // 2][:, (c % 2) * D:(c % 2 + 1) * D]

                    norm_stats(rows, b * STC + NS * 4 * NC + t * 2 * NC, s_st2)
                    dve.wait_ge(s_rs2, b * NS + t + 1)
                    dve.wait_ge(s_out, (b * NS + t) * 16 + C0)
                    norm_apply(lambda c: fin[:, c, :], rows, s_fin)

        @block.tensor
        def _(pe):
            pe.wait_ge(s_setp, 5)
            pe.wait_ge(s_setv, 15)
            pe.wait_ge(s_wlo, 4)
            pe.wait_ge(s_wo, 16)
            pe.wait_ge(s_const, 16 * len(consts))

            def three(dst, l_hi, l_lo, r_hi, r_lo):
                for k in range(KT):
                    nc.tensor.matmul(dst, l_hi(k), r_hi(k), start=(k == 0), stop=False)
                    nc.tensor.matmul(dst, l_hi(k), r_lo(k), start=False, stop=False)
                    last = nc.tensor.matmul(dst, l_lo(k), r_hi(k), start=False, stop=(k == KT - 1))
                last.then_inc(s_proj, 1)

            def project(w, p, slot):
                cols = slice(p * P, (p + 1) * P)
                three(bank[slot % 2][:], lambda k: w_hi[w][:, k, cols], lambda k: w_lo[w][:, k, cols],
                      lambda k: x_hi[:, k, :], lambda k: x_lo[:, k, :])

            with pe.Fori(0, B) as b:
                with pe.Fori(0, NS) as s:
                    it = b * NS + s
                    pe.wait_ge(s_xn, it + 1)
                    pe.wait_ge(s_att, it * NP * 2 + C0)
                    pe.wait_ge(s_fin, b * NS + C0)
                    for k in range(KT):
                        for c in range(NC):
                            last = nc.tensor.transpose(bank[2 + k][:, c * C:(c + 1) * C],
                                                       x_n[:, c, k * P:(k + 1) * P], ident[:])
                        last.then_inc(s_xt, 1)
                    pe.wait_ge(s_xlo, it + 1 + C0)
                    pe.wait_ge(s_r, it * 2 + C0)
                    for n in range(2 * NC):
                        c, half = n // 2, n % 2
                        cols = slice(half * ST, (half + 1) * ST)
                        tok = slice(c * C, (c + 1) * C)
                        if n >= 2:
                            pe.wait_ge(s_vev, it * 8 + n - 1)
                        three(bank[n % 2][:], lambda k: x_hi[:, k, tok], lambda k: x_lo[:, k, tok],
                              lambda k: w_hi["v"][:, k, cols], lambda k: w_lo["v"][:, k, cols])

                    def projections(p):
                        n = it * NP + p
                        if p == 0:
                            pe.wait_ge(s_vev, it * 8 + 7)
                        else:
                            pe.wait_ge(s_qev, n)
                        project("k", p, 3 * p)
                        if p == 0:
                            pe.wait_ge(s_vev, it * 8 + 8)
                        else:
                            pe.wait_ge(s_gev, n)
                        project("q", p, 3 * p + 1)
                        pe.wait_ge(s_kev, n + 1)
                        project("g", p, 3 * p + 2)

                    projections(0)
                    for p in range(NP):
                        n = it * NP + p
                        pe.wait_ge(s_kev, n + 1)
                        if p == 0:
                            pe.wait_ge(s_x1c, it * KT + C0)
                        pe.wait_ge(s_ktok, n + C0)
                        for c in range(NC):
                            last = nc.tensor.transpose(bank[4][:, c * C:(c + 1) * C], k_end[:, c, :], ident[:])
                        last.then_inc(s_kt, 1)
                        pe.wait_ge(s_qev, n + 1)
                        pe.wait_ge(s_att, n * 2 + C0)
                        if p == 0:
                            pe.wait_ge(s_xf, (it + 1) * KT)
                        pe.sem_inc(s_passed_pe, 1)
                        for e in range(2):
                            rows = slice(e * DH, (e + 1) * DH)
                            for c in range(NC):
                                for j in range(NB):
                                    last = nc.tensor.matmul(
                                        bank[2 + e][j * BL:(j + 1) * BL, c * C + j * BL:(c + 1) * C],
                                        k_sc[rows, c, j * BL:(j + 1) * BL], q_sb[rows, j, c, j * BL:C],
                                        start=True, stop=True)
                            last.then_inc(s_score, 1)
                        pe.wait_ge(s_ktok, n + 1 + C0)
                        pe.wait_ge(s_hs, n * (NC + 1) + C0)
                        if p == 0:
                            pe.wait_ge(s_vev, it * 8 + 8)
                        for c in range(NC):
                            for e in range(2):
                                h = 2 * p + e
                                last = nc.tensor.matmul(
                                    bank[6][e * DH:(e + 1) * DH, c * DH:(c + 1) * DH],
                                    k_tok[:, c, e * DH:(e + 1) * DH], v_sb[:, c, h * DH:(h + 1) * DH],
                                    start=True, stop=True)
                        last.then_inc(s_upd, 1)
                        if p + 1 < NP:
                            projections(p + 1)
                        pe.wait_ge(s_hbd, (n + 1) * 2 + C0)
                        pe.wait_ge(s_og, n + C0)
                        for c in range(NC):
                            nc.tensor.matmul(bank[5][:, c * C:(c + 1) * C], h_bd[:, c, :], q_sb[:, 0, c, :],
                                             start=(c == 0), stop=False, skip_group_check=True)
                        pe.wait_ge(s_att, (n + 1) * 2 + C0)
                        for c in range(NC):
                            for e in range(2):
                                h = 2 * p + e
                                last = nc.tensor.matmul(
                                    bank[5][e * DH:(e + 1) * DH, c * C:(c + 1) * C],
                                    v_sb[:, c, h * DH:(h + 1) * DH], att[:, e, c, :],
                                    start=False, stop=True, skip_group_check=True)
                        last.then_inc(s_o, 1)
                    pe.wait_ge(s_og, (it + 1) * NP + C0)
                    pe.wait_ge(s_gev, (it + 1) * NP)
                    for h in range(2):
                        for c in (2 * h, 2 * h + 1):
                            for p in range(NP):
                                last = nc.tensor.matmul(
                                    bank[h][:, (c % 2) * D:(c % 2 + 1) * D], o_g[:, p, c * C:(c + 1) * C],
                                    wo[:, p, :], start=(p == 0 and c % 2 == 0), stop=(p == NP - 1),
                                    skip_group_check=True)
                        last.then_inc(s_y, 1)
                        last = None
                    pe.wait_ge(s_x1, it + 1)
                    for k in range(KT):
                        for c in range(NC):
                            last = nc.tensor.transpose(bank[7 if k == 0 else 4][:, c * C:(c + 1) * C],
                                                       x_n[:, c, k * P:(k + 1) * P], ident[:])
                        last.then_inc(s_x1t, 1)
                pe.wait_ge(s_ms, b + 1)
                for k in range(KT):
                    last = nc.tensor.matmul(bank[7][:, 0:1], g_w1[:, k, :], msum[:, k:k + 1],
                                            start=(k == 0), stop=(k == KT - 1))
                last.then_inc(s_gp, 1)
                pe.wait_ge(s_ga, b * 3 + 1)
                nc.tensor.matmul(bank[7][0:DH, 1:2], g_w2[:], gf1[:], start=True, stop=True).then_inc(s_gp, 1)
                pe.wait_ge(s_ga, b * 3 + 2)
                nc.tensor.matmul(bank[7][:, 2:3], g_w3[:], gf2[:], start=True, stop=True).then_inc(s_gp, 1)
                for layer, n in order:
                    g = n % NG
                    v = b * VIS + n
                    if layer == 1:
                        for j in range(GT):
                            t = g * GT + j
                            src = x1t if n < NG else out_t
                            if n >= NG:
                                pe.wait_ge(s_up, (v - NG) * GT + j + 1)
                            for m in range(2):
                                if n:
                                    pe.wait_ge(s_h1, v * 4 - 4 + 2 * j + m + 1)
                                for k in range(KT):
                                    last = nc.tensor.matmul(bank[2 * j + m][:], f_w1[:, k, m * P:(m + 1) * P],
                                                            src[:, k, tile_cols(t)], start=(k == 0), stop=(k == KT - 1))
                                last.then_inc(s_l1, 1)
                    if layer == 2:
                        for j in range(GT):
                            pe.wait_ge(s_h1, v * 4 + 2 * j + 2)
                            if n:
                                pe.wait_ge(s_h2, v * GT - GT + j + 1)
                            for k in range(2):
                                last = nc.tensor.matmul(bank[4 + j][:], f_w2[:, k, :], h1[:, g * GT + j, k, :],
                                                        start=(k == 0), stop=(k == 1))
                            last.then_inc(s_l2, 1)
                    if layer == 3:
                        pe.wait_ge(s_h2, v * GT + GT)
                        if n:
                            pe.wait_ge(s_h3, v)
                        for j in range(GT):
                            last = nc.tensor.matmul(bank[6][j * DH:(j + 1) * DH, :], f_w3[:],
                                                    h2[:, g * GT + j, :], start=True, stop=True)
                        last.then_inc(s_l3, 1)
                    if layer == 4:
                        pe.wait_ge(s_h3, v + 1)
                        for j in range(GT):
                            if n or j:
                                pe.wait_ge(s_th, v * GT + j)
                            else:
                                pe.wait_ge(s_ga, b * 3 + 3)
                            rows = slice(j * DH, (j + 1) * DH)
                            nc.tensor.matmul(bank[7][:], f_w4[rows, :], h3[rows, g, :],
                                             start=True, stop=True).then_inc(s_l4, 1)
                for t in range(NS):
                    pb = 2 * (t % 2)
                    pe.wait_ge(s_y2, b * NS + t + 1)
                    if t >= 2:
                        pe.wait_ge(s_fin, b * NS + t - 1 + C0)
                    for c in range(NC):
                        for k in range(KT):
                            last = nc.tensor.transpose(
                                bank[pb + c // 2][:, (c % 2) * D + k * P:(c % 2) * D + (k + 1) * P],
                                out_t[:, k, t * ST + c * C:t * ST + (c + 1) * C], ident[:])
                    last.then_inc(s_yt, 1)


_NAMES = {
    "x": "L0_attn_x", "wq": "L0_attn_WQ", "bQ": "L0_attn_bQ", "wk": "L0_attn_WK", "bK": "L0_attn_bK",
    "wv": "L0_attn_WV", "bV": "L0_attn_bV", "wo": "L0_attn_WO", "bO": "L0_attn_bO", "wg": "L0_attn_Wg",
    "bg": "L0_attn_bg", "alpha": "L0_attn_alpha_logit", "gamma": "L0_attn_ln_gamma", "beta": "L0_attn_ln_beta",
    "cn_w1": "L0_ffn_cn_w1", "cn_b1": "L0_ffn_cn_b1", "cn_w2": "L0_ffn_cn_w2", "cn_b2": "L0_ffn_cn_b2",
    "cn_w3": "L0_ffn_cn_w3", "cn_b3": "L0_ffn_cn_b3", "cn_w4": "L0_ffn_cn_w4", "cn_b4": "L0_ffn_cn_b4",
    "gc_w1": "L0_ffn_gc_w1", "gc_b1": "L0_ffn_gc_b1", "gc_w2": "L0_ffn_gc_w2", "gc_b2": "L0_ffn_gc_b2",
    "gc_w3": "L0_ffn_gc_w3", "gc_b3": "L0_ffn_gc_b3", "range": "L0_ffn_adaptive_range",
}


def kernel(**inputs):
    import numpy as np
    import concourse.bacc as bacc
    from concourse.bass_utils import run_bass_kernel_spmd

    nc = bacc.Bacc("TRN2", target_bir_lowering=False, num_devices=1)
    arrays, args = {}, {}
    for short, name in _NAMES.items():
        v = np.asarray(inputs[name])
        if short in ("wq", "wk", "wv", "wg", "wo"):
            v = v.T
        if short in ("bQ", "bK", "bg", "alpha", "gamma", "beta", "cn_b1", "cn_b2"):
            v = v.reshape(-1, P).T
        if short == "x":
            v = v.reshape(B * T, D)
        v = np.ascontiguousarray(v)
        arrays[f"in_{short}"] = v
        args[short] = nc.dram_tensor(f"in_{short}", v.shape, mybir.dt.from_np(v.dtype), kind="ExternalInput").ap()
    out = nc.dram_tensor("out_y", (B * T, D), f32, kind="ExternalOutput").ap()
    build(nc, args, out)
    r = run_bass_kernel_spmd(nc, [arrays], core_ids=[0])
    return r.results[0]["out_y"].reshape(B, T, D)
```

```python
from contextlib import ExitStack

import concourse.bass as bass
from concourse import mybir

f32 = mybir.dt.float32
f32r = mybir.dt.float32r
i32 = mybir.dt.int32
ALU = mybir.AluOpType
ACT = mybir.ActivationFunctionType
AX = mybir.AxisListType

B, T, D = 4, 2048, 256
NH, DH = 16, 64
DI = NH * DH
P = 128
KT = D // P
NP = NH // 2
ST = 512
NS = T // ST
C = 128
NC = ST // C
BL = 32
NB = C // BL
MID = BL // 2
EPS = 1e-5
CYCLES = 3
GT = 2
NG = NS // GT
VIS = CYCLES * NG


def build(nc, a, out):
    ctx = ExitStack()
    with ctx:
        def sb(name, shape, dt=f32):
            return ctx.enter_context(nc.sbuf_tensor(name, shape, dt))

        def sem(name):
            return ctx.enter_context(nc.semaphore(name))

        w_hi = {n: sb(f"w{n}_hi", [P, KT, DI], f32r) for n in "qkvg"}
        w_lo = {n: sb(f"w{n}_lo", [P, KT, DI], f32r) for n in "qkvg"}
        wo = sb("wo", [P, NP, D])
        ident = sb("ident", [P, P])
        causal = sb("causal", [P, P])
        col_bias = sb("col_bias", [P, 3, NP])
        bias_v = sb("bias_v", [P, DI])
        bias_o = sb("bias_o", [P, D])
        gamma = sb("gamma", [P, KT])
        beta = sb("beta", [P, KT])
        NPOW = C + BL + C + 2
        logit = sb("logit", [P, NP])
        grown = sb("grown", [P, 8, NP])
        shrunk = sb("shrunk", [P, 5, NP])
        pows = sb("pows", [P, NP, NPOW])
        half_neg = sb("half_neg", [P, NC])
        f_w1 = sb("f_w1", [P, KT, D])
        f_w2 = sb("f_w2", [P, KT, P])
        f_w3 = sb("f_w3", [P, DH])
        f_w4 = sb("f_w4", [P, P])
        g_w1 = sb("g_w1", [P, KT, P])
        g_w2 = sb("g_w2", [P, DH])
        g_w3 = sb("g_w3", [DH, P])
        f_b1 = sb("f_b1", [P, KT])
        f_b2 = sb("f_b2", [P, 1])
        f_b3 = sb("f_b3", [P, 1])
        f_b4 = sb("f_b4", [P, 1])
        g_b1 = sb("g_b1", [P, 1])
        g_b2 = sb("g_b2", [DH, 1])
        g_b3 = sb("g_b3", [P, 1])
        w4c = sb("w4c", [P, 1])
        gw3c = sb("gw3c", [DH, 1])
        rng = sb("rng", [P, 1])
        rng3 = sb("rng3", [P, 1])
        rng7 = sb("rng7", [P, 1])
        sign = sb("sign", [P, KT])
        x_in = sb("x_in", [P, NC, D])
        x_nf = sb("x_nf", [P, 2, KT * ST])
        x_n = x_nf[:, 0, :].rearrange("p (c d) -> p c d", c=NC)
        x_f = x_nf[:, 1, :].rearrange("p (k n) -> p k n", k=KT)
        x_2b = sb("x_2b", [P, NC, D])
        stats = sb("stats", [P, NC, 6])
        mv = sb("mv", [P, NC, 2])
        vare = sb("vare", [P, NC])
        rstd = sb("rstd", [P, NC])
        x_hi = sb("x_hi", [P, KT, ST], f32r)
        x_lo = sb("x_lo", [P, KT, ST], f32r)
        v_sb = sb("v_sb", [P, NC, DI])
        q_sb = sb("q_sb", [P, 2, NB, NC, C])
        k_sc = sb("k_sc", [P, 2, NC, C])
        k_end = sb("k_end", [P, NC, C])
        k_tok = sb("k_tok", [P, NC, C])
        att = sb("att", [P, 2, NC, C])
        gate = sb("gate", [P, 2, ST])
        h_st = sb("h_st", [P, NP, DH])
        h_seq = sb("h_seq", [P, NC, DH])
        h_bd = sb("h_bd", [P, NC, P])
        o_g = sb("o_g", [P, NP, ST])
        x1t = sb("x1t", [P, KT, T])
        msum = sb("msum", [P, KT])
        gf1 = sb("gf1", [P, 1])
        gf2 = sb("gf2", [DH, 1])
        gf3 = sb("gf3", [P, 1])
        base = sb("base", [P, 1])
        th = sb("th", [P, ST])
        cpl = sb("cpl", [P, ST])
        shift = sb("shift", [P, NC])
        out_t = v_sb[:].rearrange("p (k c) n -> p k (c n)", k=KT)
        h1 = o_g[:].rearrange("p (t m) n -> p t m n", m=2)
        h2 = x_nf[:].rearrange("p a (t n) -> p (a t) n", n=ST)
        h3 = x_2b[:].rearrange("p (g c) d -> p g (c d)", g=NG)
        turned = x_nf[:].rearrange("p g (k n) -> p g k n", n=ST)
        fin = x_2b[:]
        w_in = out_t[:, :, 0:DI]

        bank = [ctx.enter_context(nc.psum_tensor(f"bank{n}", [P, ST], f32)) for n in range(8)]

        def part(n, k):
            return bank[n][:].rearrange("p (c n) -> p c n", c=k)

        s_const = sem("small_constants_loaded")
        s_wo = sem("wo_loaded")
        s_wdma = sem("weight_arrived")
        s_whi = sem("weight_hi_made")
        s_wlo = sem("weight_lo_made")
        s_setp = sem("pool_setup")
        s_setv = sem("vector_setup")
        s_alpha = sem("alpha_done")
        s_pow = sem("power_step")
        s_x = sem("x_loaded")
        s_xfree = sem("x_in_read")
        s_st = sem("stats_step")
        s_stats = sem("x_stats_ready")
        s_rstd = sem("x_rstd_ready")
        s_x2b = sem("x_2b_ready")
        s_xn = sem("x_n_ready")
        s_xt = sem("x_transposed")
        s_xf = sem("x_f_ready")
        s_xhi = sem("x_hi_ready")
        s_xlo = sem("x_lo_ready")
        s_v = sem("v_projected")
        s_k = sem("k_projected")
        s_q = sem("q_projected")
        s_g = sem("gate_projected")
        s_vev = sem("v_evacuated")
        s_kev = sem("k_evacuated")
        s_qev = sem("q_evacuated")
        s_gev = sem("gate_evacuated")
        s_kt = sem("k_end_transposed")
        s_ktok = sem("k_tok_ready")
        s_score = sem("scores_ready")
        s_att = sem("scores_masked")
        s_upd = sem("state_update_ready")
        s_h0 = sem("state_rows_cleared")
        s_hs = sem("state_step")
        s_hbd = sem("state_diagonal_ready")
        s_o = sem("o_ready")
        s_og = sem("o_gated")
        s_y = sem("y_ready")
        s_r = sem("residual_sum_ready")
        s_r1 = sem("ln1_stats_ready")
        s_sh = sem("ln2_shift_ready")
        s_rs1 = sem("ln1_rstd_ready")
        s_x1 = sem("x1_ready")
        s_x1t = sem("x1_transposed")
        s_x1c = sem("x1t_copied")
        s_ms = sem("mean_ready")
        s_gp = sem("global_net_product")
        s_ga = sem("global_net_activation")
        s_base = sem("base_ready")
        s_l1 = sem("layer1_ready")
        s_h1 = sem("h1_ready")
        s_l2 = sem("layer2_ready")
        s_h2 = sem("h2_ready")
        s_l3 = sem("layer3_ready")
        s_h3 = sem("h3_ready")
        s_l4 = sem("layer4_ready")
        s_th = sem("tanh_ready")
        s_cpl = sem("coupling_ready")
        s_tu = sem("turned_ready")
        s_up = sem("out_updated")
        s_y2 = sem("final_sum_ready")
        s_yt = sem("final_transposed")
        s_st2 = sem("ln2_stats_ready")
        s_rs2 = sem("ln2_rstd_ready")
        s_fin = sem("final_rows_ready")
        s_out = sem("out_stored")
        s_passed = sem("vector_passed")
        s_passed_pe = sem("tensor_passed")

        C0 = 1
        started = [s_x1, s_out, s_og, s_xlo, s_upd, s_hbd, s_o, s_x1t, s_qev, s_kev, s_hs, s_fin, s_x1c, s_ktok, s_att,
                   s_kt, s_score]

        block = ctx.enter_context(nc.Block())

        consts = [
            (col_bias[:, 0, :], a["bQ"]),
            (col_bias[:, 1, :], a["bK"]),
            (col_bias[:, 2, :], a["bg"]),
            (bias_v[:], a["bV"].unsqueeze(0).broadcast_to([P, DI])),
            (bias_o[:], a["bO"].unsqueeze(0).broadcast_to([P, D])),
            (gamma[:], a["gamma"]),
            (beta[:], a["beta"]),
            (f_w1[:], a["cn_w1"].rearrange("(k p) n -> p k n", p=P)),
            (f_w2[:], a["cn_w2"].rearrange("(k p) n -> p k n", p=P)),
            (f_w3[:], a["cn_w3"]),
            (w4c[0:DH, :], a["cn_w4"]),
            (w4c[DH:P, :], a["cn_w4"]),
            (g_w1[:], a["gc_w1"].rearrange("(k p) n -> p k n", p=P)),
            (g_w2[:], a["gc_w2"]),
            (gw3c[:], a["gc_w3"]),
            (f_b1[:], a["cn_b1"]),
            (f_b2[:], a["cn_b2"]),
            (f_b3[0:DH, :], a["cn_b3"].rearrange("(p n) -> p n", n=1)),
            (f_b3[DH:P, :], a["cn_b3"].rearrange("(p n) -> p n", n=1)),
            (f_b4[:], a["cn_b4"].unsqueeze(0).broadcast_to([P, 1])),
            (g_b1[:], a["gc_b1"].rearrange("(p n) -> p n", n=1)),
            (g_b2[:], a["gc_b2"].rearrange("(p n) -> p n", n=1)),
            (g_b3[:], a["gc_b3"].unsqueeze(0).broadcast_to([P, 1])),
            (rng[:], a["range"].unsqueeze(0).broadcast_to([P, 1])),
        ]
        x_rows = a["x"].rearrange("(i c p) d -> i p c d", c=NC, p=P)
        out_rows = out.rearrange("(i c p) d -> i p c d", c=NC, p=P)

        QP, KP, EP, HP = 0, C, C + BL, C + BL + C

        @block.sync
        def _(sp):
            for counter in started:
                sp.sem_inc(counter, C0)
            sp.dma_start(logit[:], a["alpha"]).then_inc(s_alpha, 16)
            for n, w in enumerate("qkvg"):
                if n:
                    sp.wait_ge(s_wlo, n)
                sp.dma_start(w_in, a["w" + w].rearrange("(k p) n -> p k n", p=P)).then_inc(s_wdma, 16)
            sp.dma_start(wo[:], a["wo"].rearrange("(n p) m -> p n m", p=P)).then_inc(s_wo, 16)
            sp.dma_start(x_in[:], x_rows[0]).then_inc(s_x, 16)
            with sp.Fori(0, B) as b:
                with sp.Fori(0, NS) as s:
                    it = b * NS + s
                    sp.wait_ge(s_xfree, it * 2 + 2)
                    sp.dma_start(x_in[:], x_rows[(it + 1) % (B * NS)]).then_inc(s_x, 16)
                for t in range(NS):
                    sp.wait_ge(s_fin, b * NS + t + 1 + C0)
                    sp.dma_start(out_rows[b * NS + t], fin).then_inc(s_out, 16)
            sp.wait_ge(s_out, 16 * B * NS + C0)

        @block.gpsimd
        def _(pool):
            for dst, src in consts:
                pool.dma_start(dst, src).then_inc(s_const, 16)
            nc.gpsimd.memset(ident[:], 0.0).then_inc(s_setp, 1)
            nc.gpsimd.memset(causal[:], 1.0).then_inc(s_setp, 1)
            nc.gpsimd.memset(half_neg[:], -0.5).then_inc(s_setp, 1)
            pool.wait_ge(s_setp, 3)
            nc.gpsimd.affine_select(out=ident[:], in_=ident[:], compare_op=ALU.not_equal, fill=1.0,
                                    base=0, pattern=[[-1, P]], channel_multiplier=1).then_inc(s_setp, 1)
            nc.gpsimd.affine_select(out=causal[:], in_=causal[:], compare_op=ALU.is_ge, fill=0.0,
                                    base=0, pattern=[[1, P]], channel_multiplier=-1).then_inc(s_setp, 1)
            pool.wait_ge(s_const, 16 * len(consts))
            pool.wait_ge(s_stats, 1)
            nc.gpsimd.tensor_tensor(rstd[:], vare[:], half_neg[:], ALU.pow).then_inc(s_rstd, 1)
            with pool.Fori(0, B) as b:
                with pool.Fori(0, NS) as s:
                    it = b * NS + s
                    pool.wait_ge(s_x, (it + 1) * 16)
                    pool.wait_ge(s_x1, it + C0)
                    pool.wait_ge(s_out, b * NS * 16 + C0)
                    nc.gpsimd.tensor_tensor(x_2b[:], x_in[:], bias_o[:].unsqueeze(1).broadcast_to([P, NC, D]),
                                            ALU.add).then_inc(s_x2b, 1)
                    pool.wait_ge(s_x2b, it * 2 + 1)
                    nc.gpsimd.tensor_tensor(x_2b[:], x_2b[:], x_in[:], ALU.add).then_inc(s_x2b, 1)
                    pool.wait_ge(s_x2b, it * 2 + 2)
                    pool.sem_inc(s_xfree, 1)
                    pool.wait_ge(s_stats, it + 2)
                    nc.gpsimd.tensor_tensor(rstd[:], vare[:], half_neg[:], ALU.pow).then_inc(s_rstd, 1)
                    pool.wait_ge(s_r1, it + 1)
                    nc.gpsimd.tensor_tensor(rstd[:], vare[:], half_neg[:], ALU.pow).then_inc(s_rs1, 1)
                for t in range(NS):
                    pool.wait_ge(s_st2, b * NS + t + 1)
                    nc.gpsimd.tensor_tensor(rstd[:], vare[:], half_neg[:], ALU.pow).then_inc(s_rs2, 1)

        order = []
        for r in range(CYCLES):
            g0, g1 = NG * r, NG * r + 1
            order += [(1, g0)] + ([(3, g0 - 1), (4, g0 - 1)] if r else [])
            order += [(2, g0), (3, g0), (1, g1), (4, g0), (2, g1)]
        order += [(3, VIS - 1), (4, VIS - 1)]

        def tile_cols(t):
            return slice(t * ST, (t + 1) * ST)

        @block.scalar
        def _(act):
            act.wait_ge(s_alpha, 16)
            nc.scalar.activation(grown[:, 0, :], logit[:], ACT.Sigmoid).then_inc(s_alpha, 1)
            for n, w in enumerate("qkvg"):
                act.wait_ge(s_wdma, 16 * (n + 1))
                nc.scalar.activation(w_hi[w][:], w_in, ACT.Copy).then_inc(s_whi, 1)
            act.wait_ge(s_const, 16 * len(consts))
            act.wait_ge(s_pow, 36)

            def x_parts(step, banks_of):
                for k in range(KT):
                    act.wait_ge(s_xt, step * KT + k + 1)
                    if k == 0:
                        act.wait_ge(s_xlo, step + C0)
                    nc.scalar.activation(x_f[:, k, :], bank[banks_of[k]][:], ACT.Identity,
                                         bias=beta[:, k:k + 1], scale=gamma[:, k:k + 1]).then_inc(s_xf, 1)
                act.wait_ge(s_xf, (step + 1) * KT)
                nc.scalar.activation(x_hi[:], x_f, ACT.Copy).then_inc(s_xhi, 1)

            def gate_of(p, n):
                act.wait_ge(s_g, n + 1)
                nc.scalar.activation(gate[:, p % 2, :], bank[7][:], ACT.Silu,
                                     bias=col_bias[:, 2, p:p + 1]).then_inc(s_gev, 1)

            x_parts(0, (0, 1))
            gate_of(0, 0)
            with act.Fori(0, B) as b:
                with act.Fori(0, NS) as s:
                    it = b * NS + s
                    for p in range(NP):
                        n = it * NP + p
                        act.wait_ge(s_kt, n + 1 + C0)
                        act.wait_ge(s_upd, n + C0)
                        nc.scalar.activation(k_tok[:], part(4, NC), ACT.Copy).then_inc(s_ktok, 1)
                        if p == NP - 1:
                            act.wait_ge(s_g, n + 1)
                            x_parts(it + 1, (0, 1))
                        act.wait_ge(s_hs, n * NC + NC + C0)
                        act.wait_ge(s_o, n + C0)
                        for e in range(2):
                            rows = slice(e * DH, (e + 1) * DH)
                            nc.scalar.activation(h_bd[rows, :, e * DH:(e + 1) * DH], h_seq[rows, :, :],
                                                 ACT.Copy, scale=pows[rows, p, HP:HP + 1]).then_inc(s_hbd, 1)
                        act.wait_ge(s_og, n + C0)
                        gate_of((p + 1) % NP, n + 1)
                    for k in range(KT):
                        act.wait_ge(s_x1t, it * KT + k + 1 + C0)
                        nc.scalar.activation(x1t[:, k, bass.ds(s * ST, ST)], bank[4 + k][:],
                                             ACT.Copy).then_inc(s_x1c, 1)
                act.wait_ge(s_gp, b * 3 + 1)
                nc.scalar.activation(gf1[:], bank[7][:, 0:1], ACT.Gelu, bias=g_b1[:], scale=1.0 / T).then_inc(s_ga, 1)
                act.wait_ge(s_gp, b * 3 + 2)
                nc.scalar.activation(gf2[:], bank[7][0:DH, 1:2], ACT.Gelu, bias=g_b2[:]).then_inc(s_ga, 1)
                act.wait_ge(s_gp, b * 3 + 3)
                nc.scalar.activation(gf3[:], bank[7][:, 2:3], ACT.Tanh, bias=g_b3[:], scale=0.5).then_inc(s_ga, 1)
                for layer, n in order:
                    g = n % NG
                    v = b * VIS + n
                    if layer == 1:
                        for j in range(GT):
                            for m in range(2):
                                act.wait_ge(s_l1, v * 4 + 2 * j + m + 1)
                                if n >= NG:
                                    act.wait_ge(s_l2, (v - NG) * GT + j + 1)
                                nc.scalar.activation(h1[:, g * GT + j, m, :], bank[2 * j + m][:], ACT.Gelu,
                                                     bias=f_b1[:, m:m + 1]).then_inc(s_h1, 1)
                    if layer == 2:
                        for j in range(GT):
                            act.wait_ge(s_l2, v * GT + j + 1)
                            if n >= NG:
                                act.wait_ge(s_l3, v - NG + 1)
                            nc.scalar.activation(h2[:, g * GT + j, :], bank[4 + j][:], ACT.Gelu,
                                                 bias=f_b2[:]).then_inc(s_h2, 1)
                    if layer == 3:
                        act.wait_ge(s_l3, v + 1)
                        if n >= NG:
                            act.wait_ge(s_l4, (v - NG) * GT + GT)
                        nc.scalar.activation(h3[:, g, :], bank[6][:], ACT.Gelu, bias=f_b3[:]).then_inc(s_h3, 1)
                    if layer == 4:
                        for j in range(GT):
                            act.wait_ge(s_l4, v * GT + j + 1)
                            if n or j:
                                act.wait_ge(s_cpl, v * GT + j)
                            nc.scalar.activation(th[:], bank[7][:], ACT.Tanh, bias=f_b4[:],
                                                 scale=0.5).then_inc(s_th, 1)
                for t in range(NS):
                    pb = 2 * (t % 2)
                    act.wait_ge(s_sh, b * NS + t + 1)
                    act.wait_ge(s_out, (b * NS + t) * 16 + C0)
                    for c in range(NC):
                        last = nc.scalar.activation(fin[:, c, :], bank[pb + c // 2][:, (c % 2) * D:(c % 2 + 1) * D],
                                                    ACT.Identity, bias=shift[:, c:c + 1], scale=rstd[:, c:c + 1])
                    last.then_inc(s_fin, 1)

        @block.vector
        def _(dve):
            nc.vector.memset(att[:].bitcast(i32), 0).then_inc(s_setv, 1)
            nc.vector.memset(h_bd[:].bitcast(i32), 0).then_inc(s_setv, 1)
            nc.vector.memset(bank[2][:], 0.0).then_inc(s_setv, 1)
            nc.vector.memset(bank[3][:], 0.0).then_inc(s_setv, 1)
            nc.vector.memset(sign[:], 1.0).then_inc(s_setv, 1)
            nc.vector.memset(f_w4[:], 1.0).then_inc(s_setv, 1)
            nc.vector.memset(g_w3[:], 1.0).then_inc(s_setv, 1)
            dve.wait_ge(s_setv, 7)
            nc.vector.memset(sign[DH:P, 0:1], -1.0).then_inc(s_setv, 1)
            nc.vector.memset(sign[0:DH, 1:2], -1.0).then_inc(s_setv, 1)
            dve.wait_ge(s_const, 16 * len(consts))
            nc.vector.tensor_scalar(f_w4[:], f_w4[:], w4c[:], None, ALU.mult).then_inc(s_setv, 1)
            nc.vector.tensor_scalar(g_w3[:], g_w3[:], gw3c[:], None, ALU.mult).then_inc(s_setv, 1)
            nc.vector.tensor_scalar(rng3[:], rng[:], 0.3, None, ALU.mult).then_inc(s_setv, 1)
            nc.vector.tensor_scalar(rng7[:], rng[:], 0.7, None, ALU.mult).then_inc(s_setv, 1)
            nc.vector.tensor_scalar(f_b4[:], f_b4[:], 0.5, None, ALU.mult).then_inc(s_setv, 1)
            nc.vector.tensor_scalar(g_b3[:], g_b3[:], 0.5, None, ALU.mult).then_inc(s_setv, 1)
            steps = [0]

            def link(ins):
                steps[0] += 1
                ins.then_inc(s_pow, 1)
                dve.wait_ge(s_pow, steps[0])

            dve.wait_ge(s_alpha, 17)
            link(nc.vector.reciprocal(shrunk[:, 0, :], grown[:, 0, :]))
            for n in range(7):
                link(nc.vector.tensor_tensor(grown[:, n + 1, :], grown[:, n, :], grown[:, n, :], ALU.mult))
            for n in range(4):
                link(nc.vector.tensor_tensor(shrunk[:, n + 1, :], shrunk[:, n, :], shrunk[:, n, :], ALU.mult))

            def times(dst, src, w):
                by = grown[:, w, :].unsqueeze(2).broadcast_to([P, NP, 1 << w])
                width = dst.shape[-1]
                link(nc.vector.tensor_tensor(dst, src, by[:, :, 0:width], ALU.mult))

            link(nc.vector.tensor_copy(pows[:, :, QP:QP + 1], shrunk[:, 4, :].unsqueeze(2)))
            for w in range(7):
                n = 1 << w
                times(pows[:, :, QP + n:QP + 2 * n], pows[:, :, QP:QP + n], w)
            link(nc.vector.tensor_copy(pows[:, :, KP + BL - 1:KP + BL], pows[:, :, QP + 1:QP + 2]))
            link(nc.vector.memset(pows[:, :, EP + C - 1:EP + C], 1.0))
            for w in range(5):
                n, end = 1 << w, KP + BL
                times(pows[:, :, end - 2 * n:end - n], pows[:, :, end - n:end], w)
            for w in range(7):
                n, end = 1 << w, EP + C
                times(pows[:, :, end - 2 * n:end - n], pows[:, :, end - n:end], w)
            link(nc.vector.tensor_copy(pows[:, :, HP:HP + 1], pows[:, :, QP + 2 * MID + 1:QP + 2 * MID + 2]))
            link(nc.vector.tensor_copy(pows[:, :, HP + 1:HP + 2], grown[:, 7, :].unsqueeze(2)))
            for n, w in enumerate("qkvg"):
                dve.wait_ge(s_whi, n + 1)
                nc.vector.tensor_tensor(w_lo[w][:], w_in, w_hi[w][:].bitcast(f32), ALU.subtract).then_inc(s_wlo, 1)
            dve.wait_ge(s_setv, 15)
            dve.wait_ge(s_setp, 5)

            def norm_stats(src, count, done):
                for c in range(NC):
                    nc.vector.bn_stats(stats[:, c, :], src(c)).then_inc(s_st, 1)
                dve.wait_ge(s_st, count + NC)
                dve.sem_inc(s_passed, 1)
                for c in range(NC):
                    nc.vector.bn_aggr(mv[:, c, :], stats[:, c, :]).then_inc(s_st, 1)
                dve.wait_ge(s_st, count + 2 * NC)
                nc.vector.tensor_scalar(vare[:], mv[:, :, 1], EPS, None, ALU.add).then_inc(done, 1)

            def norm_apply(dst, src, done):
                for c in range(NC):
                    last = nc.vector.tensor_scalar(dst(c), src(c), mv[:, c, 0:1], rstd[:, c:c + 1],
                                                   ALU.subtract, ALU.mult)
                last.then_inc(done, 1)

            def input_norm(step, count, free=None):
                dve.wait_ge(s_x, (step + 1) * 16)
                norm_stats(lambda c: x_in[:, c, :], count, s_stats)
                dve.wait_ge(s_rstd, step + 1)
                if free is not None:
                    dve.wait_ge(s_x1t, free)
                norm_apply(lambda c: x_n[:, c, :], lambda c: x_in[:, c, :], s_xn)
                dve.wait_ge(s_xn, step + 1)
                dve.sem_inc(s_xfree, 1)

            def low_part(step):
                dve.wait_ge(s_xhi, step + 1)
                nc.vector.tensor_tensor(x_lo[:], x_f, x_hi[:].bitcast(f32), ALU.subtract).then_inc(s_xlo, 1)

            def keys_of(p, n):
                dve.wait_ge(s_k, n + 1)
                nc.vector.scalar_tensor_tensor(
                    k_sc[:, p % 2].rearrange("p c (b r) -> p (c b) r", r=BL),
                    bank[0][:].rearrange("p (c r) -> p c r", r=BL), col_bias[:, 1, p:p + 1],
                    pows[:, p, KP:KP + BL].unsqueeze(1).broadcast_to([P, NC * NB, BL]),
                    ALU.add, ALU.mult)
                nc.vector.scalar_tensor_tensor(
                    k_end[:], part(0, NC), col_bias[:, 1, p:p + 1],
                    pows[:, p, EP:EP + C].unsqueeze(1).broadcast_to([P, NC, C]),
                    ALU.add, ALU.mult).then_inc(s_kev, 1)

            def queries_of(p, n):
                dve.wait_ge(s_q, n + 1)
                for j in range(NB):
                    last = nc.vector.scalar_tensor_tensor(
                        q_sb[:, p % 2, j, :, j * BL:C], part(1, NC)[:, :, j * BL:C], col_bias[:, 0, p:p + 1],
                        pows[:, p, QP:QP + C - j * BL].unsqueeze(1).broadcast_to([P, NC, C - j * BL]),
                        ALU.add, ALU.mult)
                last.then_inc(s_qev, 1)

            input_norm(0, 0)
            low_part(0)
            queries_of(0, 0)
            keys_of(0, 0)
            ST1 = 2 * NC
            STC = 2 * NS * ST1 + NS * ST1
            with dve.Fori(0, B) as b:
                nc.vector.memset(h_st[:], 0.0).then_inc(s_h0, 1)
                dve.wait_ge(s_h0, b + 1)
                dve.sem_inc(s_passed, 1)
                with dve.Fori(0, NS) as s:
                    it = b * NS + s
                    for m in range(2 * NC):
                        c, half = m // 2, m % 2
                        dve.wait_ge(s_v, it * 8 + m + 1)
                        cols = slice(half * ST, (half + 1) * ST)
                        nc.vector.tensor_tensor(v_sb[:, c, cols], bank[m % 2][:], bias_v[:, cols],
                                                ALU.add).then_inc(s_vev, 1)

                    def masked(e, n):
                        dve.wait_ge(s_score, n * 2 + e + 1 + C0)
                        dve.wait_ge(s_o, n + C0)
                        dve.sem_inc(s_passed, 1)
                        nc.vector.copy_predicated(
                            att[:, e], causal[:].bitcast(i32).unsqueeze(1).broadcast_to([P, NC, C]),
                            part(2 + e, NC)).then_inc(s_att, 1)

                    for p in range(NP):
                        n = it * NP + p
                        masked(0, n)
                        if p + 1 < NP:
                            dve.wait_ge(s_kt, n + 1 + C0)
                            keys_of(p + 1, n + 1)
                        dve.wait_ge(s_hbd, n * 2 + C0)
                        nc.vector.tensor_copy(h_seq[:, 0, :], h_st[:, p, :]).then_inc(s_hs, 1)
                        dve.wait_ge(s_upd, n + 1 + C0)
                        for c in range(NC):
                            dve.wait_ge(s_hs, n * NC + c + 1 + C0)
                            step = nc.vector.scalar_tensor_tensor(
                                h_seq[:, c + 1, :] if c + 1 < NC else h_st[:, p, :], h_seq[:, c, :],
                                pows[:, p, HP + 1:HP + 2], bank[6][:, c * DH:(c + 1) * DH], ALU.mult, ALU.add)
                            if c + 1 < NC:
                                step.then_inc(s_hs, 1)
                        masked(1, n)
                        if p + 1 < NP:
                            queries_of(p + 1, n + 1)
                        if p == NP - 1:
                            low_part(it + 1)
                        dve.wait_ge(s_o, n + 1 + C0)
                        dve.wait_ge(s_gev, n + 1)
                        nc.vector.tensor_tensor(o_g[:, p, :], bank[5][:], gate[:, p % 2, :],
                                                ALU.mult).then_inc(s_og, 1)
                        if p == NP - 2:
                            input_norm(it + 1, b * STC + (2 * s + 1) * ST1, it * KT + C0)
                    for h in range(2):
                        dve.wait_ge(s_y, it * 2 + h + 1)
                        dve.wait_ge(s_x2b, it * 2 + 2)
                        nc.vector.tensor_tensor(x_2b[:, 2 * h:2 * h + 2, :], x_2b[:, 2 * h:2 * h + 2, :],
                                                part(7 * (1 - h), 2), ALU.add).then_inc(s_r, 1)
                    dve.wait_ge(s_r, it * 2 + 2)
                    norm_stats(lambda c: x_2b[:, c, :], b * STC + (2 * s + 2) * ST1, s_r1)
                    dve.wait_ge(s_kt, it * NP + NP + C0)
                    queries_of(0, (it + 1) * NP)
                    dve.wait_ge(s_rs1, it + 1)
                    norm_apply(lambda c: x_n[:, c, :], lambda c: x_2b[:, c, :], s_x1)
                    keys_of(0, (it + 1) * NP)
                dve.wait_ge(s_x1c, (b + 1) * NS * KT + C0)
                nc.vector.tensor_reduce(msum[:], x1t[:], AX.X, ALU.add).then_inc(s_ms, 1)
                dve.wait_ge(s_ga, b * 3 + 3)
                nc.vector.tensor_scalar(base[:], gf3[:], rng7[:], 0.1, ALU.mult, ALU.add).then_inc(s_base, 1)
                dve.wait_ge(s_base, b + 1)
                for n in range(VIS):
                    for j in range(GT):
                        t = (n % NG) * GT + j
                        u = (b * VIS + n) * GT + j
                        src = x1t if n < NG else out_t
                        dve.wait_ge(s_th, u + 1)
                        nc.vector.tensor_scalar(cpl[:], th[:], rng3[:], base[:], ALU.mult, ALU.add).then_inc(s_cpl, 1)
                        dve.wait_ge(s_cpl, u + 1)
                        nc.vector.tensor_tensor(turned[:, n % NG, 0, :], src[:, 1, tile_cols(t)], cpl[:], ALU.mult)
                        nc.vector.tensor_tensor(turned[:, n % NG, 1, :], src[:, 0, tile_cols(t)], cpl[:],
                                                ALU.mult).then_inc(s_tu, 1)
                        dve.wait_ge(s_tu, u + 1)
                        for k in range(KT):
                            last = nc.vector.scalar_tensor_tensor(
                                out_t[:, k, tile_cols(t)], turned[:, n % NG, k, :], sign[:, k:k + 1],
                                src[:, k, tile_cols(t)], ALU.mult, ALU.add)
                        last.then_inc(s_up, 1)
                        if n >= VIS - NG:
                            dve.wait_ge(s_up, u + 1)
                            nc.vector.tensor_tensor(out_t[:, :, tile_cols(t)], out_t[:, :, tile_cols(t)],
                                                    x1t[:, :, tile_cols(t)], ALU.add).then_inc(s_y2, 1)
                for t in range(NS):
                    pb = 2 * (t % 2)
                    dve.wait_ge(s_yt, b * NS + t + 1)

                    def rows(c, pb=pb):
                        return bank[pb + c // 2][:, (c % 2) * D:(c % 2 + 1) * D]

                    if t:
                        dve.wait_ge(s_fin, b * NS + t + C0)
                    norm_stats(rows, b * STC + ST1 + 2 * NS * ST1 + t * ST1, s_st2)
                    dve.wait_ge(s_rs2, b * NS + t + 1)
                    nc.vector.scalar_tensor_tensor(shift[:], mv[:, :, 0], -1.0, rstd[:], ALU.mult,
                                                   ALU.mult).then_inc(s_sh, 1)

        @block.tensor
        def _(pe):
            pe.wait_ge(s_setp, 5)
            pe.wait_ge(s_setv, 15)
            pe.wait_ge(s_wlo, 4)
            pe.wait_ge(s_wo, 16)
            pe.wait_ge(s_const, 16 * len(consts))

            def x_transposed():
                for k in range(KT):
                    for c in range(NC):
                        last = nc.tensor.transpose(bank[k][:, c * C:(c + 1) * C],
                                                   x_n[:, c, k * P:(k + 1) * P], ident[:])
                    last.then_inc(s_xt, 1)

            def products(dst, first, end, l_hi, l_lo, r_hi, r_lo):
                for m in range(first, end):
                    k, which = m // 3, m % 3
                    l, r = ((l_hi, r_hi), (l_hi, r_lo), (l_lo, r_hi))[which]
                    last = nc.tensor.matmul(dst, l(k), r(k), start=(m == 0), stop=(m == 5))
                return last

            def project(w, p, bk, first=0, end=6):
                cols = slice(p * P, (p + 1) * P)
                return products(bank[bk][:], first, end,
                                lambda k: w_hi[w][:, k, cols], lambda k: w_lo[w][:, k, cols],
                                lambda k: x_hi[:, k, :], lambda k: x_lo[:, k, :])

            def values(m):
                c, half = m // 2, m % 2
                cols = slice(half * ST, (half + 1) * ST)
                tok = slice(c * C, (c + 1) * C)
                return products(bank[m % 2][:], 0, 6, lambda k: x_hi[:, k, tok], lambda k: x_lo[:, k, tok],
                                lambda k: w_hi["v"][:, k, cols], lambda k: w_lo["v"][:, k, cols])

            def scores(p, e, chunks):
                rows = slice(e * DH, (e + 1) * DH)
                for c in chunks:
                    for j in range(NB):
                        last = nc.tensor.matmul(
                            bank[2 + e][j * BL:(j + 1) * BL, c * C + j * BL:(c + 1) * C],
                            k_sc[rows, p % 2, c, j * BL:(j + 1) * BL], q_sb[rows, p % 2, j, c, j * BL:C],
                            start=True, stop=True)
                return last

            def y_part(h, p):
                for c in (2 * h, 2 * h + 1):
                    last = nc.tensor.matmul(
                        bank[7 * (1 - h)][:, (c % 2) * D:(c % 2 + 1) * D], o_g[:, p, c * C:(c + 1) * C],
                        wo[:, p, :], start=(p == 0 and c % 2 == 0), stop=(p == NP - 1), skip_group_check=True)
                return last

            pe.wait_ge(s_xn, 1)
            x_transposed()
            pe.wait_ge(s_xf, KT)
            pe.wait_ge(s_xlo, 1 + C0)
            project("q", 0, 1).then_inc(s_q, 1)
            project("k", 0, 0).then_inc(s_k, 1)
            project("g", 0, 7).then_inc(s_g, 1)
            with pe.Fori(0, B) as b:
                with pe.Fori(0, NS) as s:
                    it = b * NS + s
                    pe.wait_ge(s_kev, it * NP + 1 + C0)
                    pe.wait_ge(s_qev, it * NP + 1 + C0)
                    pe.wait_ge(s_fin, b * NS + C0)
                    for m in range(2 * NC):
                        if m >= 2:
                            pe.wait_ge(s_vev, it * 8 + m - 1)
                        values(m).then_inc(s_v, 1)
                    for p in range(NP):
                        n = it * NP + p
                        nxt = p + 1 < NP
                        if p == 0:
                            pe.wait_ge(s_x1c, it * KT + C0)
                        pe.wait_ge(s_kev, n + 1 + C0)
                        pe.wait_ge(s_ktok, n + C0)
                        for c in range(NC):
                            last = nc.tensor.transpose(bank[4][:, c * C:(c + 1) * C], k_end[:, c, :], ident[:])
                        last.then_inc(s_kt, 1)
                        pe.wait_ge(s_qev, n + 1 + C0)
                        pe.wait_ge(s_att, n * 2 + C0)
                        pe.sem_inc(s_passed_pe, 1)
                        scores(p, 0, (0, 1))
                        if nxt:
                            if p == 0:
                                pe.wait_ge(s_vev, it * 8 + 8)
                            project("k", p + 1, 0, 0, 4)
                        else:
                            pe.wait_ge(s_xn, it + 2)
                            x_transposed()
                        scores(p, 0, (2, 3)).then_inc(s_score, 1)
                        if nxt:
                            project("k", p + 1, 0, 4, 6).then_inc(s_k, 1)
                            project("q", p + 1, 1, 0, 2)
                        else:
                            pe.wait_ge(s_gev, n + 1)
                            for q in range(3):
                                y_part(0, q)
                        pe.wait_ge(s_ktok, n + 1 + C0)
                        for c in range(NC):
                            for e in range(2):
                                h = 2 * p + e
                                last = nc.tensor.matmul(
                                    bank[6][e * DH:(e + 1) * DH, c * DH:(c + 1) * DH],
                                    k_tok[:, c, e * DH:(e + 1) * DH], v_sb[:, c, h * DH:(h + 1) * DH],
                                    start=True, stop=True)
                        last.then_inc(s_upd, 1)
                        if nxt:
                            project("q", p + 1, 1, 2, 3)
                        scores(p, 1, (0, 1))
                        if nxt:
                            project("q", p + 1, 1, 3, 6).then_inc(s_q, 1)
                        else:
                            for q in range(3, NP - 1):
                                y_part(0, q)
                        scores(p, 1, (2, 3)).then_inc(s_score, 1)
                        if nxt:
                            pe.wait_ge(s_gev, n + 1)
                            project("g", p + 1, 7).then_inc(s_g, 1)
                        else:
                            pe.wait_ge(s_xf, it * KT + KT + 1)
                            for q in range(NP - 1):
                                y_part(1, q)
                        pe.wait_ge(s_hbd, (n + 1) * 2 + C0)
                        pe.wait_ge(s_og, n + C0)
                        for c in range(NC):
                            nc.tensor.matmul(bank[5][:, c * C:(c + 1) * C], h_bd[:, c, :], q_sb[:, p % 2, 0, c, :],
                                             start=(c == 0), stop=False, skip_group_check=True)
                        pe.wait_ge(s_att, (n + 1) * 2 + C0)
                        for c in range(NC):
                            for e in range(2):
                                h = 2 * p + e
                                last = nc.tensor.matmul(
                                    bank[5][e * DH:(e + 1) * DH, c * C:(c + 1) * C],
                                    v_sb[:, c, h * DH:(h + 1) * DH], att[:, e, c, :],
                                    start=False, stop=True, skip_group_check=True)
                        last.then_inc(s_o, 1)
                    pe.wait_ge(s_xlo, it + 2 + C0)
                    pe.wait_ge(s_xf, (it + 2) * KT)
                    project("q", 0, 1).then_inc(s_q, 1)
                    pe.wait_ge(s_og, (it + 1) * NP + C0)
                    for h in range(2):
                        y_part(h, NP - 1).then_inc(s_y, 1)
                    pe.wait_ge(s_r, it * 2 + 1)
                    project("g", 0, 7).then_inc(s_g, 1)
                    pe.wait_ge(s_r, it * 2 + 2)
                    project("k", 0, 0).then_inc(s_k, 1)
                    pe.wait_ge(s_x1, it + 1 + C0)
                    for k in range(KT):
                        for c in range(NC):
                            last = nc.tensor.transpose(bank[4 + k][:, c * C:(c + 1) * C],
                                                       x_n[:, c, k * P:(k + 1) * P], ident[:])
                        last.then_inc(s_x1t, 1)
                pe.wait_ge(s_kev, (b + 1) * NS * NP + 1 + C0)
                pe.wait_ge(s_qev, (b + 1) * NS * NP + 1 + C0)
                pe.wait_ge(s_gev, (b + 1) * NS * NP + 1)
                pe.wait_ge(s_x1c, (b + 1) * NS * KT + C0)
                pe.wait_ge(s_ms, b + 1)
                for k in range(KT):
                    last = nc.tensor.matmul(bank[7][:, 0:1], g_w1[:, k, :], msum[:, k:k + 1],
                                            start=(k == 0), stop=(k == KT - 1))
                last.then_inc(s_gp, 1)
                pe.wait_ge(s_ga, b * 3 + 1)
                nc.tensor.matmul(bank[7][0:DH, 1:2], g_w2[:], gf1[:], start=True, stop=True).then_inc(s_gp, 1)
                pe.wait_ge(s_ga, b * 3 + 2)
                nc.tensor.matmul(bank[7][:, 2:3], g_w3[:], gf2[:], start=True, stop=True).then_inc(s_gp, 1)
                for layer, n in order:
                    g = n % NG
                    v = b * VIS + n
                    if layer == 1:
                        for j in range(GT):
                            t = g * GT + j
                            src = x1t if n < NG else out_t
                            if n >= NG:
                                pe.wait_ge(s_up, (v - NG) * GT + j + 1)
                            for m in range(2):
                                if n:
                                    pe.wait_ge(s_h1, v * 4 - 4 + 2 * j + m + 1)
                                for k in range(KT):
                                    last = nc.tensor.matmul(bank[2 * j + m][:], f_w1[:, k, m * P:(m + 1) * P],
                                                            src[:, k, tile_cols(t)], start=(k == 0), stop=(k == KT - 1))
                                last.then_inc(s_l1, 1)
                    if layer == 2:
                        for j in range(GT):
                            pe.wait_ge(s_h1, v * 4 + 2 * j + 2)
                            if n:
                                pe.wait_ge(s_h2, v * GT - GT + j + 1)
                            for k in range(2):
                                last = nc.tensor.matmul(bank[4 + j][:], f_w2[:, k, :], h1[:, g * GT + j, k, :],
                                                        start=(k == 0), stop=(k == 1))
                            last.then_inc(s_l2, 1)
                    if layer == 3:
                        pe.wait_ge(s_h2, v * GT + GT)
                        if n:
                            pe.wait_ge(s_h3, v)
                        for j in range(GT):
                            last = nc.tensor.matmul(bank[6][j * DH:(j + 1) * DH, :], f_w3[:],
                                                    h2[:, g * GT + j, :], start=True, stop=True)
                        last.then_inc(s_l3, 1)
                    if layer == 4:
                        pe.wait_ge(s_h3, v + 1)
                        for j in range(GT):
                            if n or j:
                                pe.wait_ge(s_th, v * GT + j)
                            else:
                                pe.wait_ge(s_ga, b * 3 + 3)
                            rows = slice(j * DH, (j + 1) * DH)
                            nc.tensor.matmul(bank[7][:], f_w4[rows, :], h3[rows, g, :],
                                             start=True, stop=True).then_inc(s_l4, 1)
                for t in range(NS):
                    pb = 2 * (t % 2)
                    pe.wait_ge(s_y2, b * NS + t + 1)
                    if t >= 2:
                        pe.wait_ge(s_fin, b * NS + t - 1 + C0)
                    for c in range(NC):
                        for k in range(KT):
                            last = nc.tensor.transpose(
                                bank[pb + c // 2][:, (c % 2) * D + k * P:(c % 2) * D + (k + 1) * P],
                                out_t[:, k, t * ST + c * C:t * ST + (c + 1) * C], ident[:])
                    last.then_inc(s_yt, 1)


_NAMES = {
    "x": "L0_attn_x", "wq": "L0_attn_WQ", "bQ": "L0_attn_bQ", "wk": "L0_attn_WK", "bK": "L0_attn_bK",
    "wv": "L0_attn_WV", "bV": "L0_attn_bV", "wo": "L0_attn_WO", "bO": "L0_attn_bO", "wg": "L0_attn_Wg",
    "bg": "L0_attn_bg", "alpha": "L0_attn_alpha_logit", "gamma": "L0_attn_ln_gamma", "beta": "L0_attn_ln_beta",
    "cn_w1": "L0_ffn_cn_w1", "cn_b1": "L0_ffn_cn_b1", "cn_w2": "L0_ffn_cn_w2", "cn_b2": "L0_ffn_cn_b2",
    "cn_w3": "L0_ffn_cn_w3", "cn_b3": "L0_ffn_cn_b3", "cn_w4": "L0_ffn_cn_w4", "cn_b4": "L0_ffn_cn_b4",
    "gc_w1": "L0_ffn_gc_w1", "gc_b1": "L0_ffn_gc_b1", "gc_w2": "L0_ffn_gc_w2", "gc_b2": "L0_ffn_gc_b2",
    "gc_w3": "L0_ffn_gc_w3", "gc_b3": "L0_ffn_gc_b3", "range": "L0_ffn_adaptive_range",
}


def kernel(**inputs):
    import numpy as np
    import concourse.bacc as bacc
    from concourse.bass_utils import run_bass_kernel_spmd

    nc = bacc.Bacc("TRN2", target_bir_lowering=False, num_devices=1)
    arrays, args = {}, {}
    for short, name in _NAMES.items():
        v = np.asarray(inputs[name])
        if short in ("wq", "wk", "wv", "wg", "wo"):
            v = v.T
        if short in ("bQ", "bK", "bg", "alpha", "gamma", "beta", "cn_b1", "cn_b2"):
            v = v.reshape(-1, P).T
        if short == "x":
            v = v.reshape(B * T, D)
        v = np.ascontiguousarray(v)
        arrays[f"in_{short}"] = v
        args[short] = nc.dram_tensor(f"in_{short}", v.shape, mybir.dt.from_np(v.dtype), kind="ExternalInput").ap()
    out = nc.dram_tensor("out_y", (B * T, D), f32, kind="ExternalOutput").ap()
    build(nc, args, out)
    r = run_bass_kernel_spmd(nc, [arrays], core_ids=[0])
    return r.results[0]["out_y"].reshape(B, T, D)
```

```python
from contextlib import ExitStack

import concourse.bass as bass
from concourse import mybir

f32 = mybir.dt.float32
f32r = mybir.dt.float32r
i32 = mybir.dt.int32
ALU = mybir.AluOpType
ACT = mybir.ActivationFunctionType
AX = mybir.AxisListType

B, T, D = 4, 2048, 256
NH, DH = 16, 64
DI = NH * DH
P = 128
KT = D // P
NP = NH // 2
ST = 512
NS = T // ST
C = 128
NC = ST // C
BL = 32
NB = C // BL
MID = BL // 2
EPS = 1e-5
CYCLES = 3
GT = 2
NG = NS // GT
VIS = CYCLES * NG


def build(nc, a, out):
    ctx = ExitStack()
    with ctx:
        def sb(name, shape, dt=f32):
            return ctx.enter_context(nc.sbuf_tensor(name, shape, dt))

        def sem(name):
            return ctx.enter_context(nc.semaphore(name))

        w_hi = {n: sb(f"w{n}_hi", [P, KT, DI], f32r) for n in "qkvg"}
        w_lo = {n: sb(f"w{n}_lo", [P, KT, DI], f32r) for n in "qkvg"}
        wo = sb("wo", [P, NP, D])
        ident = sb("ident", [P, P])
        causal = sb("causal", [P, P])
        col_bias = sb("col_bias", [P, 3, NP])
        bias_v = sb("bias_v", [P, DI])
        bias_o = sb("bias_o", [P, D])
        gamma = sb("gamma", [P, KT])
        beta = sb("beta", [P, KT])
        NPOW = C + BL + C + 2
        logit = sb("logit", [P, NP])
        grown = sb("grown", [P, 8, NP])
        shrunk = sb("shrunk", [P, 5, NP])
        pows = sb("pows", [P, NP, NPOW])
        half_neg = sb("half_neg", [P, NC])
        f_w1 = sb("f_w1", [P, KT, D])
        f_w2 = sb("f_w2", [P, KT, P])
        f_w3 = sb("f_w3", [P, DH])
        f_w4 = sb("f_w4", [P, P])
        g_w1 = sb("g_w1", [P, KT, P])
        g_w2 = sb("g_w2", [P, DH])
        g_w3 = sb("g_w3", [DH, P])
        f_b1 = sb("f_b1", [P, KT])
        f_b2 = sb("f_b2", [P, 1])
        f_b3 = sb("f_b3", [P, 1])
        f_b4 = sb("f_b4", [P, 1])
        g_b1 = sb("g_b1", [P, 1])
        g_b2 = sb("g_b2", [DH, 1])
        g_b3 = sb("g_b3", [P, 1])
        w4c = sb("w4c", [P, 1])
        gw3c = sb("gw3c", [DH, 1])
        rng = sb("rng", [P, 1])
        rng3 = sb("rng3", [P, 1])
        rng7 = sb("rng7", [P, 1])
        sign = sb("sign", [P, KT])
        x_in = sb("x_in", [P, NC, D])
        x_nf = sb("x_nf", [P, 2, KT * ST])
        x_n = x_nf[:, 0, :].rearrange("p (c d) -> p c d", c=NC)
        x_f = x_nf[:, 1, :].rearrange("p (k n) -> p k n", k=KT)
        x_2b = sb("x_2b", [P, NC, D])
        stats = sb("stats", [P, NC, 6])
        mv = sb("mv", [P, NC, 2])
        vare = sb("vare", [P, NC])
        rstd = sb("rstd", [P, NC])
        x_hi = sb("x_hi", [P, KT, ST], f32r)
        x_lo = sb("x_lo", [P, KT, ST], f32r)
        v_sb = sb("v_sb", [P, NC, DI])
        q_sb = sb("q_sb", [P, 2, NB, NC, C])
        k_sc = sb("k_sc", [P, 2, NC, C])
        k_end = sb("k_end", [P, NC, C])
        k_tok = sb("k_tok", [P, NC, C])
        att = sb("att", [P, 2, NC, C])
        gate = sb("gate", [P, 2, ST])
        h_st = sb("h_st", [P, NP, DH])
        h_seq = sb("h_seq", [P, NC, DH])
        h_bd = sb("h_bd", [P, NC, P])
        o_g = sb("o_g", [P, NP, ST])
        x1t = sb("x1t", [P, KT, T])
        msum = sb("msum", [P, 2, KT])
        gf1 = sb("gf1", [P, 1])
        gf2 = sb("gf2", [DH, 1])
        gf3 = sb("gf3", [P, 1])
        base = sb("base", [P, 1])
        th = sb("th", [P, ST])
        cpl = sb("cpl", [P, ST])
        mv2 = sb("mv2", [P, NS, NC, 2])
        vare2 = sb("vare2", [P, NS, NC])
        rstd2 = sb("rstd2", [P, NS, NC])
        shift = sb("shift", [P, NS, NC])
        out_t = v_sb[:].rearrange("p (k c) n -> p k (c n)", k=KT)
        h1 = o_g[:].rearrange("p (t m) n -> p t m n", m=2)
        h2 = x_nf[:].rearrange("p a (t n) -> p (a t) n", n=ST)
        h3 = x_2b[:].rearrange("p (g c) d -> p g (c d)", g=NG)
        turned = x_nf[:].rearrange("p g (k n) -> p g k n", n=ST)
        fin = o_g[:].rearrange("p (t m) (c d) -> p t (m c) d", t=NS, d=D)
        v_rows = v_sb[:].rearrange("p c (h n) -> p (c h) n", n=ST)
        w_in = [tile.rearrange("p (i k h) n -> p i k (h n)", i=2, k=KT)[:, i] for tile in (v_rows, o_g[:]) for i in range(2)]

        bank = [ctx.enter_context(nc.psum_tensor(f"bank{n}", [P, ST], f32)) for n in range(8)]

        def part(n, k):
            return bank[n][:].rearrange("p (c n) -> p c n", c=k)

        s_const = sem("small_constants_loaded")
        s_first = sem("first_constants_loaded")
        s_wo = sem("wo_loaded")
        s_wdma = [sem(f"weight_{w}_arrived") for w in "qkgv"]
        s_whi = sem("weight_hi_made")
        s_wlo = [sem(f"weight_{w}_lo_made") for w in "qkgv"]
        s_setp = sem("pool_setup")
        s_setv = sem("vector_setup")
        s_alpha = sem("alpha_done")
        s_pow = sem("power_step")
        s_x = sem("x_loaded")
        s_xfree = sem("x_in_read")
        s_st = sem("stats_step")
        s_stats = sem("x_stats_ready")
        s_rstd = sem("x_rstd_ready")
        s_x2b = sem("x_2b_ready")
        s_xn = sem("x_n_ready")
        s_xt = sem("x_transposed")
        s_xf = sem("x_f_ready")
        s_xhi = sem("x_hi_ready")
        s_xlo = sem("x_lo_ready")
        s_v = sem("v_projected")
        s_k = sem("k_projected")
        s_q = sem("q_projected")
        s_g = sem("gate_projected")
        s_vev = sem("v_evacuated")
        s_kev = sem("k_evacuated")
        s_qev = sem("q_evacuated")
        s_gev = sem("gate_evacuated")
        s_kt = sem("k_end_transposed")
        s_ktok = sem("k_tok_ready")
        s_score = sem("scores_ready")
        s_att = sem("scores_masked")
        s_upd = sem("state_update_ready")
        s_h0 = sem("state_rows_cleared")
        s_hs = sem("state_step")
        s_hbd = sem("state_diagonal_ready")
        s_o = sem("o_ready")
        s_og = sem("o_gated")
        s_y = sem("y_ready")
        s_r = sem("residual_sum_ready")
        s_r1 = sem("ln1_stats_ready")
        s_sh = sem("ln2_shift_ready")
        s_rs1 = sem("ln1_rstd_ready")
        s_x1 = sem("x1_ready")
        s_x1t = sem("x1_transposed")
        s_x1c = sem("x1t_copied")
        s_ms = sem("mean_ready")
        s_gp = sem("global_net_product")
        s_ga = sem("global_net_activation")
        s_base = sem("base_ready")
        s_l1 = sem("layer1_ready")
        s_h1 = sem("h1_ready")
        s_l2 = sem("layer2_ready")
        s_h2 = sem("h2_ready")
        s_l3 = sem("layer3_ready")
        s_h3 = sem("h3_ready")
        s_l4 = sem("layer4_ready")
        s_th = sem("tanh_ready")
        s_cpl = sem("coupling_ready")
        s_tu = sem("turned_ready")
        s_up = sem("out_updated")
        s_pre = sem("x1_plus_result_ready")
        s_y2 = sem("final_sum_ready")
        s_yt = sem("final_transposed")
        s_st2 = sem("ln2_stats_ready")
        s_rs2 = sem("ln2_rstd_ready")
        s_fin = sem("final_rows_ready")
        s_out = sem("out_stored")
        s_passed = sem("vector_passed")
        s_passed_pe = sem("tensor_passed")

        C0 = 1
        CF = 4
        started = [s_x1, s_out, s_og, s_xlo, s_upd, s_hbd, s_o, s_x1t, s_qev, s_kev, s_hs, s_x1c, s_ktok, s_att,
                   s_kt, s_score]

        block = ctx.enter_context(nc.Block())

        first_consts = [
            (gamma[:], a["gamma"]),
            (beta[:], a["beta"]),
            (col_bias[:, 0, :], a["bQ"]),
            (col_bias[:, 1, :], a["bK"]),
            (col_bias[:, 2, :], a["bg"]),
        ]
        consts = [
            (bias_v[:], a["bV"].unsqueeze(0).broadcast_to([P, DI])),
            (bias_o[:], a["bO"].unsqueeze(0).broadcast_to([P, D])),
            (f_w1[:], a["cn_w1"].rearrange("(k p) n -> p k n", p=P)),
            (f_w2[:], a["cn_w2"].rearrange("(k p) n -> p k n", p=P)),
            (f_w3[:], a["cn_w3"]),
            (w4c[0:DH, :], a["cn_w4"]),
            (w4c[DH:P, :], a["cn_w4"]),
            (g_w1[:], a["gc_w1"].rearrange("(k p) n -> p k n", p=P)),
            (g_w2[:], a["gc_w2"]),
            (gw3c[:], a["gc_w3"]),
            (f_b1[:], a["cn_b1"]),
            (f_b2[:], a["cn_b2"]),
            (f_b3[0:DH, :], a["cn_b3"].rearrange("(p n) -> p n", n=1)),
            (f_b3[DH:P, :], a["cn_b3"].rearrange("(p n) -> p n", n=1)),
            (f_b4[:], a["cn_b4"].unsqueeze(0).broadcast_to([P, 1])),
            (g_b1[:], a["gc_b1"].rearrange("(p n) -> p n", n=1)),
            (g_b2[:], a["gc_b2"].rearrange("(p n) -> p n", n=1)),
            (g_b3[:], a["gc_b3"].unsqueeze(0).broadcast_to([P, 1])),
            (rng[:], a["range"].unsqueeze(0).broadcast_to([P, 1])),
        ]
        x_rows = a["x"].rearrange("(i c p) d -> i p c d", c=NC, p=P)
        out_rows = out.rearrange("(i c p) d -> i p c d", c=NC, p=P)

        QP, KP, EP, HP = 0, C, C + BL, C + BL + C

        def load_weight(engine, n):
            engine.dma_start(w_in[n], a["w" + "qkgv"[n]].rearrange("(k p) n -> p k n", p=P)).then_inc(s_wdma[n], 16)

        @block.sync
        def _(sp):
            for counter in started:
                sp.sem_inc(counter, C0)
            sp.sem_inc(s_fin, CF)
            sp.dma_start(x_in[:], x_rows[0]).then_inc(s_x, 16)
            for dst, src in first_consts:
                sp.dma_start(dst, src).then_inc(s_first, 16)
            load_weight(sp, 1)
            for dst, src in consts:
                sp.dma_start(dst, src).then_inc(s_const, 16)
            with sp.Fori(0, B) as b:
                with sp.Fori(0, NS) as s:
                    it = b * NS + s
                    sp.wait_ge(s_xfree, it * 2 + 2)
                    sp.dma_start(x_in[:], x_rows[(it + 1) % (B * NS)]).then_inc(s_x, 16)
                for t in range(NS):
                    sp.wait_ge(s_fin, b * NS + t + 1 + CF)
                    sp.dma_start(out_rows[b * NS + t], fin[:, t]).then_inc(s_out, 16)
            sp.wait_ge(s_out, 16 * B * NS + C0)

        order = [(1, 0, range(GT))]
        for n in range(VIS):
            more = n + 1 < VIS
            order += [(2, n, range(GT))] + [(1, n + 1, [0])] * more + [(3, n, range(GT))] + [(1, n + 1, [1])] * more
            order += [(4, n, range(GT))]

        def tile_cols(t):
            return slice(t * ST, (t + 1) * ST)

        def up_count(b, n, j):
            return (b * (VIS - NG) + n) * GT + j + 1

        def final_rows(t, c):
            return bank[(2, 0, 4, 6)[t] + c // 2][:, (c % 2) * D:(c % 2 + 1) * D]

        def v_bank(m):
            return bank[(2, 3, 1, 4, 5, 6, 7, 0)[m]]

        def l1_bank(j, m):
            return bank[2 * (1 - j) + m]

        @block.gpsimd
        def _(pool):
            nc.gpsimd.memset(ident[:], 0.0).then_inc(s_setp, 1)
            nc.gpsimd.memset(causal[:], 1.0).then_inc(s_setp, 1)
            nc.gpsimd.memset(half_neg[:], -0.5).then_inc(s_setp, 1)
            pool.wait_ge(s_setp, 3)
            nc.gpsimd.affine_select(out=ident[:], in_=ident[:], compare_op=ALU.not_equal, fill=1.0,
                                    base=0, pattern=[[-1, P]], channel_multiplier=1).then_inc(s_setp, 1)
            nc.gpsimd.affine_select(out=causal[:], in_=causal[:], compare_op=ALU.is_ge, fill=0.0,
                                    base=0, pattern=[[1, P]], channel_multiplier=-1).then_inc(s_setp, 1)
            pool.wait_ge(s_stats, 1)
            nc.gpsimd.tensor_tensor(rstd[:], vare[:], half_neg[:], ALU.pow).then_inc(s_rstd, 1)
            for n, w in ((2, "g"), (3, "v")):
                pool.wait_ge(s_whi, n + 1)
                nc.gpsimd.tensor_tensor(w_lo[w][:], w_in[n], w_hi[w][:].bitcast(f32), ALU.subtract).then_inc(s_wlo[n], 1)
            pool.wait_ge(s_const, 16 * len(consts))
            with pool.Fori(0, B) as b:
                with pool.Fori(0, NS) as s:
                    it = b * NS + s
                    pool.wait_ge(s_x, (it + 1) * 16)
                    pool.wait_ge(s_x1, it + C0)
                    nc.gpsimd.tensor_tensor(x_2b[:], x_in[:], bias_o[:].unsqueeze(1).broadcast_to([P, NC, D]),
                                            ALU.add).then_inc(s_x2b, 1)
                    pool.wait_ge(s_x2b, it * 2 + 1)
                    nc.gpsimd.tensor_tensor(x_2b[:], x_2b[:], x_in[:], ALU.add).then_inc(s_x2b, 1)
                    pool.wait_ge(s_x2b, it * 2 + 2)
                    pool.sem_inc(s_xfree, 1)
                    pool.wait_ge(s_stats, it + 2)
                    nc.gpsimd.tensor_tensor(rstd[:], vare[:], half_neg[:], ALU.pow).then_inc(s_rstd, 1)
                    pool.wait_ge(s_r1, it + 1)
                    nc.gpsimd.tensor_tensor(rstd[:], vare[:], half_neg[:], ALU.pow).then_inc(s_rs1, 1)
                for t in range(NS):
                    pool.wait_ge(s_up, up_count(b, VIS - 2 * NG, t))
                    nc.gpsimd.tensor_tensor(x1t[:, :, tile_cols(t)], x1t[:, :, tile_cols(t)],
                                            out_t[:, :, tile_cols(t)], ALU.add).then_inc(s_pre, 1)
                for t in range(NS):
                    pool.wait_ge(s_st2, b * NS + t + 1)
                    nc.gpsimd.tensor_tensor(rstd2[:, t], vare2[:, t], half_neg[:], ALU.pow).then_inc(s_rs2, 1)

        @block.scalar
        def _(act):
            act.dma_start(logit[:], a["alpha"]).then_inc(s_alpha, 16)
            load_weight(act, 0)
            act.wait_ge(s_alpha, 16)
            nc.scalar.activation(grown[:, 0, :], logit[:], ACT.Sigmoid).then_inc(s_alpha, 1)

            def weight_high(n, w):
                act.wait_ge(s_wdma[n], 16)
                nc.scalar.activation(w_hi[w][:], w_in[n], ACT.Copy).then_inc(s_whi, 1)

            def x_parts(step, banks_of):
                for k in range(KT):
                    act.wait_ge(s_xt, step * KT + k + 1)
                    if k == 0:
                        act.wait_ge(s_xlo, step + C0)
                    nc.scalar.activation(x_f[:, k, :], bank[banks_of[k]][:], ACT.Identity,
                                         bias=beta[:, k:k + 1], scale=gamma[:, k:k + 1]).then_inc(s_xf, 1)
                act.wait_ge(s_xf, (step + 1) * KT)
                nc.scalar.activation(x_hi[:], x_f, ACT.Copy).then_inc(s_xhi, 1)

            def gate_of(p, n):
                act.wait_ge(s_g, n + 1)
                nc.scalar.activation(gate[:, p % 2, :], bank[7][:], ACT.Silu,
                                     bias=col_bias[:, 2, p:p + 1]).then_inc(s_gev, 1)

            def x1_copied(b, s, place):
                for k in range(KT):
                    act.wait_ge(s_x1t, (b * (NS + 1) + s) * KT + k + 1 + C0)
                    nc.scalar.activation(x1t[:, k, bass.ds(place * ST, ST)], bank[4 + k][:],
                                         ACT.Copy).then_inc(s_x1c, 1)

            def global_net(b, layer):
                act.wait_ge(s_gp, b * 3 + layer)
                if layer == 1:
                    ins = nc.scalar.activation(gf1[:], bank[7][:, 0:1], ACT.Gelu, bias=g_b1[:], scale=1.0 / T)
                elif layer == 2:
                    ins = nc.scalar.activation(gf2[:], bank[7][0:DH, 1:2], ACT.Gelu, bias=g_b2[:])
                else:
                    ins = nc.scalar.activation(gf3[:], bank[7][:, 2:3], ACT.Tanh, bias=g_b3[:], scale=0.5)
                ins.then_inc(s_ga, 1)

            weight_high(0, "q")
            load_weight(act, 2)
            load_weight(act, 3)
            act.dma_start(wo[:], a["wo"].rearrange("(n p) m -> p n m", p=P)).then_inc(s_wo, 16)
            act.wait_ge(s_first, 16 * len(first_consts))
            x_parts(0, (0, 1))
            for n, w in enumerate("kgv"):
                weight_high(n + 1, w)
            gate_of(0, 0)
            act.wait_ge(s_const, 16 * len(consts))
            act.wait_ge(s_pow, 36)
            with act.Fori(0, B) as b:
                with act.Fori(0, NS) as s:
                    it = b * NS + s
                    x1_copied(b, s, (s + NS - 1) % NS)
                    for p in range(NP):
                        n = it * NP + p
                        act.wait_ge(s_kt, n + 1 + C0)
                        act.wait_ge(s_upd, n + C0)
                        nc.scalar.activation(k_tok[:], part(4, NC), ACT.Copy).then_inc(s_ktok, 1)
                        if p == NP - 1:
                            act.wait_ge(s_g, n + 1)
                            x_parts(it + 1, (0, 1))
                        act.wait_ge(s_hs, n * NC + NC + C0)
                        act.wait_ge(s_o, n + C0)
                        for e in range(2):
                            rows = slice(e * DH, (e + 1) * DH)
                            nc.scalar.activation(h_bd[rows, :, e * DH:(e + 1) * DH], h_seq[rows, :, :],
                                                 ACT.Copy, scale=pows[rows, p, HP:HP + 1]).then_inc(s_hbd, 1)
                        act.wait_ge(s_og, n + C0)
                        gate_of((p + 1) % NP, n + 1)
                for layer, n, tiles in order:
                    g = n % NG
                    v = b * VIS + n
                    if layer == 1:
                        for j in tiles:
                            for m in range(2):
                                act.wait_ge(s_l1, v * 4 + 2 * j + m + 1)
                                if n >= NG:
                                    act.wait_ge(s_l2, (v - NG) * GT + j + 1)
                                nc.scalar.activation(h1[:, g * GT + j, m, :], l1_bank(j, m)[:], ACT.Gelu,
                                                     bias=f_b1[:, m:m + 1]).then_inc(s_h1, 1)
                        if n == 0:
                            x1_copied(b, NS, NS - 1)
                        if n == 1 and 0 in tiles:
                            global_net(b, 2)
                    if layer == 2:
                        for j in range(GT):
                            act.wait_ge(s_l2, v * GT + j + 1)
                            if n >= NG:
                                act.wait_ge(s_l3, v - NG + 1)
                            nc.scalar.activation(h2[:, g * GT + j, :], bank[4 + j][:], ACT.Gelu,
                                                 bias=f_b2[:]).then_inc(s_h2, 1)
                        if n == 0:
                            global_net(b, 1)
                    if layer == 3:
                        act.wait_ge(s_l3, v + 1)
                        if n >= NG:
                            act.wait_ge(s_l4, (v - NG) * GT + GT)
                        nc.scalar.activation(h3[:, g, :], bank[6][:], ACT.Gelu, bias=f_b3[:]).then_inc(s_h3, 1)
                        if n == 0:
                            global_net(b, 3)
                    if layer == 4:
                        for j in range(GT):
                            act.wait_ge(s_l4, v * GT + j + 1)
                            if n or j:
                                act.wait_ge(s_cpl, v * GT + j)
                            nc.scalar.activation(th[:], bank[7 - j][:], ACT.Tanh, bias=f_b4[:],
                                                 scale=0.5).then_inc(s_th, 1)
                for t in range(NS):
                    act.wait_ge(s_sh, b * NS + t + 1)
                    for c in range(NC):
                        last = nc.scalar.activation(fin[:, t, c, :], final_rows(t, c), ACT.Identity,
                                                    bias=shift[:, t, c:c + 1], scale=rstd2[:, t, c:c + 1])
                    last.then_inc(s_fin, 1)

        @block.vector
        def _(dve):
            nc.vector.memset(att[:].bitcast(i32), 0).then_inc(s_setv, 1)
            nc.vector.memset(h_bd[:].bitcast(i32), 0).then_inc(s_setv, 1)
            nc.vector.memset(bank[2][:], 0.0).then_inc(s_setv, 1)
            nc.vector.memset(bank[3][:], 0.0).then_inc(s_setv, 1)
            nc.vector.memset(sign[:], 1.0).then_inc(s_setv, 1)
            nc.vector.memset(f_w4[:], 1.0).then_inc(s_setv, 1)
            nc.vector.memset(g_w3[:], 1.0).then_inc(s_setv, 1)
            dve.wait_ge(s_setv, 7)
            nc.vector.memset(sign[DH:P, 0:1], -1.0).then_inc(s_setv, 1)
            nc.vector.memset(sign[0:DH, 1:2], -1.0).then_inc(s_setv, 1)
            def weight_low(n, w):
                dve.wait_ge(s_whi, n + 1)
                nc.vector.tensor_tensor(w_lo[w][:], w_in[n], w_hi[w][:].bitcast(f32),
                                        ALU.subtract).then_inc(s_wlo[n], 1)

            dve.wait_ge(s_setp, 5)

            def norm_stats(src, count, done, mv=mv[:], vare=vare[:]):
                for c in range(NC):
                    nc.vector.bn_stats(stats[:, c, :], src(c)).then_inc(s_st, 1)
                dve.wait_ge(s_st, count + NC)
                dve.sem_inc(s_passed, 1)
                for c in range(NC):
                    nc.vector.bn_aggr(mv[:, c, :], stats[:, c, :]).then_inc(s_st, 1)
                dve.wait_ge(s_st, count + 2 * NC)
                nc.vector.tensor_scalar(vare, mv[:, :, 1], EPS, None, ALU.add).then_inc(done, 1)

            def norm_apply(dst, src, done):
                for c in range(NC):
                    last = nc.vector.tensor_scalar(dst(c), src(c), mv[:, c, 0:1], rstd[:, c:c + 1],
                                                   ALU.subtract, ALU.mult)
                last.then_inc(done, 1)

            def input_stats(step, count):
                dve.wait_ge(s_x, (step + 1) * 16)
                norm_stats(lambda c: x_in[:, c, :], count, s_stats)

            def input_norm(step, free=None):
                dve.wait_ge(s_rstd, step + 1)
                if free is not None:
                    dve.wait_ge(s_x1t, free)
                norm_apply(lambda c: x_n[:, c, :], lambda c: x_in[:, c, :], s_xn)
                dve.wait_ge(s_xn, step + 1)
                dve.sem_inc(s_xfree, 1)

            def low_part(step):
                dve.wait_ge(s_xhi, step + 1)
                nc.vector.tensor_tensor(x_lo[:], x_f, x_hi[:].bitcast(f32), ALU.subtract).then_inc(s_xlo, 1)

            def keys_of(p, n):
                dve.wait_ge(s_k, n + 1)
                nc.vector.scalar_tensor_tensor(
                    k_sc[:, p % 2].rearrange("p c (b r) -> p (c b) r", r=BL),
                    bank[0][:].rearrange("p (c r) -> p c r", r=BL), col_bias[:, 1, p:p + 1],
                    pows[:, p, KP:KP + BL].unsqueeze(1).broadcast_to([P, NC * NB, BL]),
                    ALU.add, ALU.mult)
                nc.vector.scalar_tensor_tensor(
                    k_end[:], part(0, NC), col_bias[:, 1, p:p + 1],
                    pows[:, p, EP:EP + C].unsqueeze(1).broadcast_to([P, NC, C]),
                    ALU.add, ALU.mult).then_inc(s_kev, 1)

            def queries_of(p, n):
                dve.wait_ge(s_q, n + 1)
                for j in range(NB):
                    last = nc.vector.scalar_tensor_tensor(
                        q_sb[:, p % 2, j, :, j * BL:C], part(1, NC)[:, :, j * BL:C], col_bias[:, 0, p:p + 1],
                        pows[:, p, QP:QP + C - j * BL].unsqueeze(1).broadcast_to([P, NC, C - j * BL]),
                        ALU.add, ALU.mult)
                last.then_inc(s_qev, 1)

            steps = [0]

            def link(ins):
                steps[0] += 1
                ins.then_inc(s_pow, 1)
                dve.wait_ge(s_pow, steps[0])

            dve.wait_ge(s_alpha, 17)
            link(nc.vector.reciprocal(shrunk[:, 0, :], grown[:, 0, :]))
            for n in range(7):
                link(nc.vector.tensor_tensor(grown[:, n + 1, :], grown[:, n, :], grown[:, n, :], ALU.mult))
            for n in range(4):
                link(nc.vector.tensor_tensor(shrunk[:, n + 1, :], shrunk[:, n, :], shrunk[:, n, :], ALU.mult))

            input_stats(0, 0)
            input_norm(0)
            weight_low(0, "q")
            def times(dst, src, w):
                by = grown[:, w, :].unsqueeze(2).broadcast_to([P, NP, 1 << w])
                width = dst.shape[-1]
                link(nc.vector.tensor_tensor(dst, src, by[:, :, 0:width], ALU.mult))

            link(nc.vector.tensor_copy(pows[:, :, QP:QP + 1], shrunk[:, 4, :].unsqueeze(2)))
            for w in range(7):
                n = 1 << w
                times(pows[:, :, QP + n:QP + 2 * n], pows[:, :, QP:QP + n], w)
            low_part(0)
            weight_low(1, "k")
            link(nc.vector.tensor_copy(pows[:, :, KP + BL - 1:KP + BL], pows[:, :, QP + 1:QP + 2]))
            link(nc.vector.memset(pows[:, :, EP + C - 1:EP + C], 1.0))
            for w in range(5):
                n, end = 1 << w, KP + BL
                times(pows[:, :, end - 2 * n:end - n], pows[:, :, end - n:end], w)
            for w in range(7):
                n, end = 1 << w, EP + C
                times(pows[:, :, end - 2 * n:end - n], pows[:, :, end - n:end], w)
            link(nc.vector.tensor_copy(pows[:, :, HP:HP + 1], pows[:, :, QP + 2 * MID + 1:QP + 2 * MID + 2]))
            link(nc.vector.tensor_copy(pows[:, :, HP + 1:HP + 2], grown[:, 7, :].unsqueeze(2)))
            dve.wait_ge(s_const, 16 * len(consts))
            nc.vector.tensor_scalar(f_w4[:], f_w4[:], w4c[:], None, ALU.mult).then_inc(s_setv, 1)
            nc.vector.tensor_scalar(g_w3[:], g_w3[:], gw3c[:], None, ALU.mult).then_inc(s_setv, 1)
            nc.vector.tensor_scalar(rng3[:], rng[:], 0.3, None, ALU.mult).then_inc(s_setv, 1)
            nc.vector.tensor_scalar(rng7[:], rng[:], 0.7, None, ALU.mult).then_inc(s_setv, 1)
            nc.vector.tensor_scalar(f_b4[:], f_b4[:], 0.5, None, ALU.mult).then_inc(s_setv, 1)
            nc.vector.tensor_scalar(g_b3[:], g_b3[:], 0.5, None, ALU.mult).then_inc(s_setv, 1)
            dve.wait_ge(s_first, 16 * len(first_consts))
            queries_of(0, 0)
            keys_of(0, 0)
            ST1 = 2 * NC
            STC = 2 * NS * ST1 + NS * ST1
            with dve.Fori(0, B) as b:
                nc.vector.memset(h_st[:], 0.0).then_inc(s_h0, 1)
                dve.wait_ge(s_h0, b + 1)
                dve.sem_inc(s_passed, 1)
                with dve.Fori(0, NS) as s:
                    it = b * NS + s
                    for m in range(2 * NC):
                        c, half = m // 2, m % 2
                        dve.wait_ge(s_v, it * 2 * NC + m + 1)
                        cols = slice(half * ST, (half + 1) * ST)
                        nc.vector.tensor_tensor(v_sb[:, c, cols], v_bank(m)[:], bias_v[:, cols],
                                                ALU.add).then_inc(s_vev, 1)

                    def masked(e, n):
                        dve.wait_ge(s_score, n * 2 + e + 1 + C0)
                        dve.wait_ge(s_o, n + C0)
                        dve.sem_inc(s_passed, 1)
                        nc.vector.copy_predicated(
                            att[:, e], causal[:].bitcast(i32).unsqueeze(1).broadcast_to([P, NC, C]),
                            part(2 + e, NC)).then_inc(s_att, 1)

                    for p in range(NP):
                        n = it * NP + p
                        masked(0, n)
                        dve.wait_ge(s_hbd, n * 2 + C0)
                        nc.vector.tensor_copy(h_seq[:, 0, :], h_st[:, p, :]).then_inc(s_hs, 1)
                        dve.wait_ge(s_upd, n + 1 + C0)
                        for c in range(NC):
                            dve.wait_ge(s_hs, n * NC + c + 1 + C0)
                            step = nc.vector.scalar_tensor_tensor(
                                h_seq[:, c + 1, :] if c + 1 < NC else h_st[:, p, :], h_seq[:, c, :],
                                pows[:, p, HP + 1:HP + 2], bank[6][:, c * DH:(c + 1) * DH], ALU.mult, ALU.add)
                            if c + 1 < NC:
                                step.then_inc(s_hs, 1)
                        masked(1, n)
                        if p + 1 < NP:
                            dve.wait_ge(s_kt, n + 1 + C0)
                            keys_of(p + 1, n + 1)
                            queries_of(p + 1, n + 1)
                        if p == NP - 1:
                            low_part(it + 1)
                        dve.wait_ge(s_o, n + 1 + C0)
                        dve.wait_ge(s_gev, n + 1)
                        if p == 0:
                            dve.wait_ge(s_out, b * NS * 16 + C0)
                        nc.vector.tensor_tensor(o_g[:, p, :], bank[5][:], gate[:, p % 2, :],
                                                ALU.mult).then_inc(s_og, 1)
                        if p == NP - 5:
                            input_stats(it + 1, b * STC + (2 * s + 1) * ST1)
                        if p == NP - 3:
                            input_norm(it + 1, (b * (NS + 1) + s + 1) * KT + C0)
                    for h in range(2):
                        dve.wait_ge(s_y, it * 2 + h + 1)
                        dve.wait_ge(s_x2b, it * 2 + 2)
                        nc.vector.tensor_tensor(x_2b[:, 2 * h:2 * h + 2, :], x_2b[:, 2 * h:2 * h + 2, :],
                                                part(7 * (1 - h), 2), ALU.add).then_inc(s_r, 1)
                    dve.wait_ge(s_r, it * 2 + 2)
                    norm_stats(lambda c: x_2b[:, c, :], b * STC + (2 * s + 2) * ST1, s_r1)
                    dve.wait_ge(s_kt, it * NP + NP + C0)
                    queries_of(0, (it + 1) * NP)
                    keys_of(0, (it + 1) * NP)
                    dve.wait_ge(s_rs1, it + 1)
                    norm_apply(lambda c: x_n[:, c, :], lambda c: x_2b[:, c, :], s_x1)
                for n, (first, end) in enumerate(((0, T - ST), (T - ST, T))):
                    dve.wait_ge(s_x1c, (b * (NS + 1) + NS + n) * KT + C0)
                    nc.vector.tensor_reduce(msum[:, n, :], x1t[:, :, first:end], AX.X, ALU.add).then_inc(s_ms, 1)
                dve.wait_ge(s_ga, b * 3 + 3)
                nc.vector.tensor_scalar(base[:], gf3[:], rng7[:], 0.1, ALU.mult, ALU.add).then_inc(s_base, 1)
                dve.wait_ge(s_base, b + 1)

                def final_stats(t):
                    dve.wait_ge(s_yt, b * NS + t + 1)
                    norm_stats(lambda c: final_rows(t, c), b * STC + ST1 + 2 * NS * ST1 + t * ST1, s_st2,
                               mv2[:, t], vare2[:, t])

                def final_shift(t):
                    dve.wait_ge(s_rs2, b * NS + t + 1)
                    nc.vector.scalar_tensor_tensor(shift[:, t], mv2[:, t, :, 0], -1.0, rstd2[:, t], ALU.mult,
                                                   ALU.mult).then_inc(s_sh, 1)

                for n in range(VIS):
                    for j in range(GT):
                        t = (n % NG) * GT + j
                        u = (b * VIS + n) * GT + j
                        src = x1t if n < NG else out_t
                        final = n >= VIS - NG
                        dve.wait_ge(s_th, u + 1)
                        nc.vector.tensor_scalar(cpl[:], th[:], rng3[:], base[:], ALU.mult, ALU.add).then_inc(s_cpl, 1)
                        dve.wait_ge(s_cpl, u + 1)
                        for k in range(KT):
                            nc.vector.tensor_tensor(turned[:, n % NG, k, :], src[:, 1 - k, tile_cols(t)], cpl[:],
                                                    ALU.mult).then_inc(s_tu, 1)
                        if final:
                            dve.wait_ge(s_pre, b * NS + t + 1)
                            src = x1t
                        for k in range(KT):
                            dve.wait_ge(s_tu, u * KT + KT)
                            last = nc.vector.scalar_tensor_tensor(
                                out_t[:, k, tile_cols(t)], turned[:, n % NG, k, :], sign[:, k:k + 1],
                                src[:, k, tile_cols(t)], ALU.mult, ALU.add)
                        last.then_inc(s_y2 if final else s_up, 1)
                        if n == VIS - 1 and j == 0:
                            final_stats(1)
                            final_shift(0)
                    if n == VIS - NG:
                        final_stats(0)
                final_shift(1)
                for t in (2, 3):
                    final_stats(t)
                for t in (2, 3):
                    final_shift(t)

        @block.tensor
        def _(pe):
            pe.wait_ge(s_setp, 5)
            def x_transposed():
                for k in range(KT):
                    for c in range(NC):
                        last = nc.tensor.transpose(bank[k][:, c * C:(c + 1) * C],
                                                   x_n[:, c, k * P:(k + 1) * P], ident[:])
                    last.then_inc(s_xt, 1)

            def products(dst, first, end, l_hi, l_lo, r_hi, r_lo):
                for m in range(first, end):
                    k, which = m // 3, m % 3
                    l, r = ((l_hi, r_hi), (l_hi, r_lo), (l_lo, r_hi))[which]
                    last = nc.tensor.matmul(dst, l(k), r(k), start=(m == 0), stop=(m == 5))
                return last

            def project(w, p, bk, first=0, end=6):
                cols = slice(p * P, (p + 1) * P)
                return products(bank[bk][:], first, end,
                                lambda k: w_hi[w][:, k, cols], lambda k: w_lo[w][:, k, cols],
                                lambda k: x_hi[:, k, :], lambda k: x_lo[:, k, :])

            def values(m):
                c, half = m // 2, m % 2
                cols = slice(half * ST, (half + 1) * ST)
                tok = slice(c * C, (c + 1) * C)
                return products(v_bank(m)[:], 0, 6, lambda k: x_hi[:, k, tok], lambda k: x_lo[:, k, tok],
                                lambda k: w_hi["v"][:, k, cols], lambda k: w_lo["v"][:, k, cols])

            def scores(p, e, chunks):
                rows = slice(e * DH, (e + 1) * DH)
                for c in chunks:
                    for j in range(NB):
                        last = nc.tensor.matmul(
                            bank[2 + e][j * BL:(j + 1) * BL, c * C + j * BL:(c + 1) * C],
                            k_sc[rows, p % 2, c, j * BL:(j + 1) * BL], q_sb[rows, p % 2, j, c, j * BL:C],
                            start=True, stop=True)
                return last

            def y_part(h, p):
                for c in (2 * h, 2 * h + 1):
                    last = nc.tensor.matmul(
                        bank[7 * (1 - h)][:, (c % 2) * D:(c % 2 + 1) * D], o_g[:, p, c * C:(c + 1) * C],
                        wo[:, p, :], start=(p == 0 and c % 2 == 0), stop=(p == NP - 1), skip_group_check=True)
                return last

            def x1_transposed(steps):
                pe.wait_ge(s_x1, steps + C0)
                for k in range(KT):
                    for c in range(NC):
                        last = nc.tensor.transpose(bank[4 + k][:, c * C:(c + 1) * C],
                                                   x_n[:, c, k * P:(k + 1) * P], ident[:])
                    last.then_inc(s_x1t, 1)

            def final_transposed(b, t):
                pe.wait_ge(s_y2, b * NS + t + 1)
                for c in range(NC):
                    for k in range(KT):
                        last = nc.tensor.transpose(final_rows(t, c)[:, k * P:(k + 1) * P],
                                                   out_t[:, k, t * ST + c * C:t * ST + (c + 1) * C], ident[:])
                last.then_inc(s_yt, 1)

            pe.wait_ge(s_xn, 1)
            x_transposed()
            pe.wait_ge(s_xf, KT)
            for n, (w, bk, done) in enumerate((("q", 1, s_q), ("k", 0, s_k), ("g", 7, s_g))):
                pe.wait_ge(s_wlo[n], 1)
                pe.wait_ge(s_xlo, 1 + C0)
                project(w, 0, bk).then_inc(done, 1)
            pe.wait_ge(s_wlo[3], 1)
            with pe.Fori(0, B) as b:
                with pe.Fori(0, NS) as s:
                    it = b * NS + s
                    pe.wait_ge(s_att, it * NP * 2 + C0)
                    pe.wait_ge(s_fin, b * NS - 3 + CF)
                    for m in range(2 * NC):
                        if m == 2:
                            pe.wait_ge(s_qev, it * NP + 1 + C0)
                            pe.wait_ge(s_fin, b * NS - 2 + CF)
                        if m == 3:
                            pe.wait_ge(s_ktok, it * NP + C0)
                            pe.wait_ge(s_fin, b * NS - 1 + CF)
                        if m == 4:
                            pe.wait_ge(s_og, it * NP + C0)
                        if m == 5:
                            pe.wait_ge(s_fin, b * NS + CF)
                        if m == 6:
                            pe.wait_ge(s_gev, it * NP + 1)
                        if m == 7:
                            pe.wait_ge(s_kev, it * NP + 1 + C0)
                        values(m).then_inc(s_v, 1)
                        if m == 5:
                            pe.wait_ge(s_vev, it * 2 * NC + 5)
                            x1_transposed(it)
                    pe.wait_ge(s_wo, 16)
                    pe.wait_ge(s_setv, 15)
                    pe.wait_ge(s_const, 16 * len(consts))
                    for p in range(NP):
                        n = it * NP + p
                        nxt = p + 1 < NP
                        if p == 0:
                            pe.wait_ge(s_x1c, (b * (NS + 1) + s + 1) * KT + C0)
                        pe.wait_ge(s_kev, n + 1 + C0)
                        pe.wait_ge(s_ktok, n + C0)
                        for c in range(NC):
                            last = nc.tensor.transpose(bank[4][:, c * C:(c + 1) * C], k_end[:, c, :], ident[:])
                        last.then_inc(s_kt, 1)
                        pe.wait_ge(s_qev, n + 1 + C0)
                        pe.wait_ge(s_att, n * 2 + C0)
                        pe.sem_inc(s_passed_pe, 1)
                        scores(p, 0, range(NC)).then_inc(s_score, 1)
                        if p == 0:
                            pe.wait_ge(s_vev, it * 2 * NC + 2 * NC)
                        pe.wait_ge(s_ktok, n + 1 + C0)
                        for c in range(NC):
                            for e in range(2):
                                h = 2 * p + e
                                last = nc.tensor.matmul(
                                    bank[6][e * DH:(e + 1) * DH, c * DH:(c + 1) * DH],
                                    k_tok[:, c, e * DH:(e + 1) * DH], v_sb[:, c, h * DH:(h + 1) * DH],
                                    start=True, stop=True)
                        last.then_inc(s_upd, 1)
                        scores(p, 1, range(NC)).then_inc(s_score, 1)
                        if nxt:
                            project("k", p + 1, 0).then_inc(s_k, 1)
                        else:
                            pe.wait_ge(s_xn, it + 2)
                            x_transposed()
                        if nxt:
                            project("q", p + 1, 1).then_inc(s_q, 1)
                        else:
                            pe.wait_ge(s_gev, n + 1)
                            pe.wait_ge(s_og, n + C0)
                            for q in range(NP - 1):
                                y_part(0, q)
                        if nxt:
                            pe.wait_ge(s_gev, n + 1)
                            project("g", p + 1, 7).then_inc(s_g, 1)
                        else:
                            pe.wait_ge(s_xf, it * KT + KT + 1)
                            for q in range(NP - 1):
                                y_part(1, q)
                        pe.wait_ge(s_hbd, (n + 1) * 2 + C0)
                        pe.wait_ge(s_og, n + C0)
                        for c in range(NC):
                            nc.tensor.matmul(bank[5][:, c * C:(c + 1) * C], h_bd[:, c, :], q_sb[:, p % 2, 0, c, :],
                                             start=(c == 0), stop=False, skip_group_check=True)
                        pe.wait_ge(s_att, (n + 1) * 2 + C0)
                        for c in range(NC):
                            for e in range(2):
                                h = 2 * p + e
                                last = nc.tensor.matmul(
                                    bank[5][e * DH:(e + 1) * DH, c * C:(c + 1) * C],
                                    v_sb[:, c, h * DH:(h + 1) * DH], att[:, e, c, :],
                                    start=False, stop=True, skip_group_check=True)
                        last.then_inc(s_o, 1)
                    pe.wait_ge(s_xlo, it + 2 + C0)
                    pe.wait_ge(s_xf, (it + 2) * KT)
                    project("q", 0, 1).then_inc(s_q, 1)
                    pe.wait_ge(s_og, (it + 1) * NP + C0)
                    for h in range(2):
                        y_part(h, NP - 1).then_inc(s_y, 1)
                    pe.wait_ge(s_r, it * 2 + 1)
                    project("g", 0, 7).then_inc(s_g, 1)
                    pe.wait_ge(s_r, it * 2 + 2)
                    project("k", 0, 0).then_inc(s_k, 1)
                def global_net(b, layer):
                    if layer == 1:
                        for n in range(2):
                            pe.wait_ge(s_ms, b * 2 + n + 1)
                            for k in range(KT):
                                last = nc.tensor.matmul(bank[7][:, 0:1], g_w1[:, k, :], msum[:, n, k:k + 1],
                                                        start=(n == 0 and k == 0), stop=(n == 1 and k == KT - 1))
                    else:
                        pe.wait_ge(s_ga, b * 3 + layer - 1)
                        if layer == 2:
                            last = nc.tensor.matmul(bank[7][0:DH, 1:2], g_w2[:], gf1[:], start=True, stop=True)
                        else:
                            last = nc.tensor.matmul(bank[7][:, 2:3], g_w3[:], gf2[:], start=True, stop=True)
                    last.then_inc(s_gp, 1)

                for layer, n, tiles in order:
                    g = n % NG
                    v = b * VIS + n
                    if layer == 1:
                        for j in tiles:
                            t = g * GT + j
                            src = x1t if n < NG else out_t
                            if n == 0 and j == 0:
                                pe.wait_ge(s_att, (b + 1) * NS * NP * 2 + C0)
                            if n == 0 and j == 1:
                                pe.wait_ge(s_kev, (b + 1) * NS * NP + 1 + C0)
                                pe.wait_ge(s_qev, (b + 1) * NS * NP + 1 + C0)
                            if n >= NG:
                                pe.wait_ge(s_up, up_count(b, n - NG, j))
                            for m in range(2):
                                if n:
                                    pe.wait_ge(s_h1, v * 4 - 4 + 2 * j + m + 1)
                                for k in range(KT):
                                    last = nc.tensor.matmul(l1_bank(j, m)[:], f_w1[:, k, m * P:(m + 1) * P],
                                                            src[:, k, tile_cols(t)], start=(k == 0), stop=(k == KT - 1))
                                last.then_inc(s_l1, 1)
                        if n == 1 and 0 in tiles:
                            global_net(b, 2)
                        if n == 0:
                            pe.wait_ge(s_ktok, (b + 1) * NS * NP + C0)
                            pe.wait_ge(s_og, (b + 1) * NS * NP + C0)
                            x1_transposed((b + 1) * NS)
                    if layer == 2:
                        for j in tiles:
                            if n == 0:
                                pe.wait_ge(s_x1c, (b + 1) * (NS + 1) * KT - 1 + j + C0)
                            pe.wait_ge(s_h1, v * 4 + 2 * j + 2)
                            if n:
                                pe.wait_ge(s_h2, v * GT - GT + j + 1)
                            for k in range(2):
                                last = nc.tensor.matmul(bank[4 + j][:], f_w2[:, k, :], h1[:, g * GT + j, k, :],
                                                        start=(k == 0), stop=(k == 1))
                            last.then_inc(s_l2, 1)
                        if n == 0:
                            pe.wait_ge(s_gev, (b + 1) * NS * NP + 1)
                            global_net(b, 1)
                    if layer == 3:
                        if n == VIS - 1:
                            final_transposed(b, 0)
                        pe.wait_ge(s_h2, v * GT + GT)
                        if n:
                            pe.wait_ge(s_th, v * GT)
                        for j in tiles:
                            last = nc.tensor.matmul(bank[6][j * DH:(j + 1) * DH, :], f_w3[:],
                                                    h2[:, g * GT + j, :], start=True, stop=True)
                        last.then_inc(s_l3, 1)
                        if n == 0:
                            global_net(b, 3)
                    if layer == 4:
                        if n == 0:
                            pe.wait_ge(s_ga, b * 3 + 3)
                        pe.wait_ge(s_h3, v + 1)
                        for j in tiles:
                            if n and j == 0:
                                pe.wait_ge(s_th, v * GT - 1)
                            rows = slice(j * DH, (j + 1) * DH)
                            nc.tensor.matmul(bank[7 - j][:], f_w4[rows, :], h3[rows, g, :],
                                             start=True, stop=True).then_inc(s_l4, 1)
                for t in range(1, NS):
                    final_transposed(b, t)


_NAMES = {
    "x": "L0_attn_x", "wq": "L0_attn_WQ", "bQ": "L0_attn_bQ", "wk": "L0_attn_WK", "bK": "L0_attn_bK",
    "wv": "L0_attn_WV", "bV": "L0_attn_bV", "wo": "L0_attn_WO", "bO": "L0_attn_bO", "wg": "L0_attn_Wg",
    "bg": "L0_attn_bg", "alpha": "L0_attn_alpha_logit", "gamma": "L0_attn_ln_gamma", "beta": "L0_attn_ln_beta",
    "cn_w1": "L0_ffn_cn_w1", "cn_b1": "L0_ffn_cn_b1", "cn_w2": "L0_ffn_cn_w2", "cn_b2": "L0_ffn_cn_b2",
    "cn_w3": "L0_ffn_cn_w3", "cn_b3": "L0_ffn_cn_b3", "cn_w4": "L0_ffn_cn_w4", "cn_b4": "L0_ffn_cn_b4",
    "gc_w1": "L0_ffn_gc_w1", "gc_b1": "L0_ffn_gc_b1", "gc_w2": "L0_ffn_gc_w2", "gc_b2": "L0_ffn_gc_b2",
    "gc_w3": "L0_ffn_gc_w3", "gc_b3": "L0_ffn_gc_b3", "range": "L0_ffn_adaptive_range",
}


def kernel(**inputs):
    import numpy as np
    import concourse.bacc as bacc
    from concourse.bass_utils import run_bass_kernel_spmd

    nc = bacc.Bacc("TRN2", target_bir_lowering=False, num_devices=1)
    arrays, args = {}, {}
    for short, name in _NAMES.items():
        v = np.asarray(inputs[name])
        if short in ("wq", "wk", "wv", "wg", "wo"):
            v = v.T
        if short in ("bQ", "bK", "bg", "alpha", "gamma", "beta", "cn_b1", "cn_b2"):
            v = v.reshape(-1, P).T
        if short == "x":
            v = v.reshape(B * T, D)
        v = np.ascontiguousarray(v)
        arrays[f"in_{short}"] = v
        args[short] = nc.dram_tensor(f"in_{short}", v.shape, mybir.dt.from_np(v.dtype), kind="ExternalInput").ap()
    out = nc.dram_tensor("out_y", (B * T, D), f32, kind="ExternalOutput").ap()
    build(nc, args, out)
    r = run_bass_kernel_spmd(nc, [arrays], core_ids=[0])
    return r.results[0]["out_y"].reshape(B, T, D)
```
